# Optimizing a Trainium2 kernel written in Bass

```python
import numpy as np
import jax
import jax.numpy as jnp

def _softmax(x, axis=-1):
    return jax.nn.softmax(x, axis=axis)

def _gelu(x):
    return jax.nn.gelu(x, approximate=True)

def _silu(x):
    return jax.nn.silu(x)

def _sigmoid(x):
    return jax.nn.sigmoid(x)

def _layernorm(x, axis=-1, eps=1e-05):
    m = jnp.mean(x, axis=axis, keepdims=True)
    v = jnp.var(x, axis=axis, keepdims=True)
    return (x - m) / jnp.sqrt(v + eps)

def _scatter_add(tgt, idx, src, axis=0):
    return tgt.at[idx].add(src)

def _segment_sum(src, seg, n):
    return jax.ops.segment_sum(src, seg, n)
kernel_name = 'mk_flamingo_gated_d1_seqx_r2_90e205'

def setup_inputs(seed: int=0):
    np.random.seed(seed)
    _w = jnp.asarray

    def _rec_inputs():
        import jax
        import jax.numpy as jnp
        _rk = jax.random.key(seed)
        x = -0.0002928 + 1 * jax.random.normal(jax.random.fold_in(_rk, 1), (4, 1024, 512), jnp.float32)
        _lenS = 1024 - jax.random.randint(jax.random.fold_in(_rk, 7), (4,), 0, max(1, 1024 // 4) + 1, jnp.int32)
        _lenS2 = 1024 - jax.random.randint(jax.random.fold_in(_rk, 8), (4,), 0, max(1, 1024 // 4) + 1, jnp.int32)
        _ctx_1024P = jax.random.normal(jax.random.fold_in(_rk, 11), (4, 16, 512), jnp.float32)
        _ctx_1024c = jax.random.dirichlet(jax.random.fold_in(_rk, 511), 0.3 * jnp.ones((16,), jnp.float32), (4, 1024))
        _ctx_1024t = jnp.einsum('bsk,bkd->bsd', _ctx_1024c, _ctx_1024P)
        _ctx_1024t = _ctx_1024t * jax.lax.rsqrt(jnp.mean(jnp.square(_ctx_1024t)) + 1e-12) * 0.953939
        ctx_1024 = -1.39393e-06 + 0.999914 * (_ctx_1024t + 0.3 * jax.random.normal(jax.random.fold_in(_rk, 611), (4, 1024, 512), jnp.float32))
        _validS = jnp.arange(1024)[None, :] < _lenS[:, None]
        _validS2 = jnp.arange(1024)[None, :] < _lenS2[:, None]
        _causal = jnp.tril(jnp.ones((1024, 1024), dtype=bool))
        mask_Bx1xSxS2_ik1 = jnp.where(jnp.broadcast_to(_validS2[:, None, None, :], (4, 1, 1024, 1024)), 1, 0).astype(jnp.int32)
        _g = jax.random.normal(jax.random.fold_in(_rk, 9001), (2, 1), jnp.float32)
        _g = jnp.sign(_g) * jnp.maximum(jnp.abs(_g), 1.0) + (_g == 0) * 1.0
        g_xattn = _g[0]
        g_ffn = _g[1]
        return (x, ctx_1024, mask_Bx1xSxS2_ik1, g_xattn, g_ffn)
    x, ctx_1024, mask_Bx1xSxS2_ik1, g_xattn, g_ffn = _rec_inputs()

    def _L0_xattn_setup():
        import jax, jax.numpy as jnp
        import numpy as np
        B, S, E, H = (2, 1024, 512, 16)
        D = E // H
        key = jax.random.key(seed)
        ks = jax.random.split(key, 14)
        inp = {'query': jax.random.normal(ks[0], (B, S, E), jnp.float32), 'key': jax.random.normal(ks[1], (B, S, E), jnp.float32), 'value': jax.random.normal(ks[2], (B, S, E), jnp.float32), 'adj': jax.random.normal(ks[3], (S, S), jnp.float32), 'mask': jax.random.randint(ks[4], (B, 1, S, S), 0, 2, jnp.int32)}
        sc = 1.0 / np.sqrt(E)
        inp['Wq'] = jax.random.normal(ks[5], (E, E), jnp.float32) * sc
        inp['bq'] = jax.random.normal(ks[6], (E,), jnp.float32) * sc
        inp['Wk'] = jax.random.normal(ks[7], (E, E), jnp.float32) * sc
        inp['bk'] = jax.random.normal(ks[8], (E,), jnp.float32) * sc
        inp['Wv'] = jax.random.normal(ks[9], (E, E), jnp.float32) * sc
        inp['bv'] = jax.random.normal(ks[10], (E,), jnp.float32) * sc
        inp['Wo'] = jax.random.normal(ks[11], (E, E), jnp.float32) * sc
        inp['bo'] = jax.random.normal(ks[12], (E,), jnp.float32) * sc
        return inp
    _L0_xattn_all = _L0_xattn_setup()
    _L0_xattn_in = {k: v for k, v in _L0_xattn_all.items() if k in ('adj', 'Wq', 'bq', 'Wk', 'bk', 'Wv', 'bv', 'Wo', 'bo')}
    del _L0_xattn_all

    def _L0_ffn_setup():
        import jax, jax.numpy as jnp
        import numpy as np
        B, S, DIM = (4, 2048, 512)
        BASE_COUPLING = 0.1
        NUM_CYCLES = 3

        def _gelu(x):
            return jax.nn.gelu(x, approximate=False)

        def _coupling_net(h, w1, b1, w2, b2, w3, b3, w4, b4):
            h = _gelu(h @ w1 + b1)
            h = _gelu(h @ w2 + b2)
            h = _gelu(h @ w3 + b3)
            return jax.nn.sigmoid(h @ w4 + b4)

        def _global_net(h, w1, b1, w2, b2, w3, b3):
            h = _gelu(h @ w1 + b1)
            h = _gelu(h @ w2 + b2)
            return jax.nn.sigmoid(h @ w3 + b3)

        def _twist(x):
            o_r, o_i, p_r, p_i = jnp.split(x, 4, axis=-1)
            return jnp.concatenate([p_r, -p_i, -o_r, o_i], axis=-1)
        key = jax.random.key(seed)
        ks = jax.random.split(key, 9)
        d = DIM

        def w(k, fan_in, fan_out):
            return jax.random.normal(k, (fan_in, fan_out), dtype=jnp.float32) / np.sqrt(fan_in).astype(np.float32)
        inp = {'x': jax.random.normal(ks[0], (B, S, d), dtype=jnp.float32)}
        cn_dims = [(d, d), (d, d // 2), (d // 2, d // 4), (d // 4, 1)]
        for i, (a, b) in enumerate(cn_dims):
            inp[f'cn_w{i + 1}'] = w(ks[1 + i], a, b)
            inp[f'cn_b{i + 1}'] = jnp.zeros((b,), dtype=jnp.float32)
        gc_dims = [(d, d // 2), (d // 2, d // 4), (d // 4, 1)]
        for i, (a, b) in enumerate(gc_dims):
            inp[f'gc_w{i + 1}'] = w(ks[5 + i], a, b)
            inp[f'gc_b{i + 1}'] = jnp.zeros((b,), dtype=jnp.float32)
        inp['adaptive_range'] = jnp.full((1,), 0.2, dtype=jnp.float32)
        return inp
    _L0_ffn_all = _L0_ffn_setup()
    _L0_ffn_in = {k: v for k, v in _L0_ffn_all.items() if k in ('cn_w1', 'cn_b1', 'cn_w2', 'cn_b2', 'cn_w3', 'cn_b3', 'cn_w4', 'cn_b4', 'gc_w1', 'gc_b1', 'gc_w2', 'gc_b2', 'gc_w3', 'gc_b3', 'adaptive_range')}
    del _L0_ffn_all
    return {'x': x, 'ctx_1024': ctx_1024, 'mask_Bx1xSxS2_ik1': mask_Bx1xSxS2_ik1, 'g_xattn': g_xattn, 'g_ffn': g_ffn, 'L0_xattn_adj': _L0_xattn_in['adj'], 'L0_xattn_Wq': _L0_xattn_in['Wq'], 'L0_xattn_bq': _L0_xattn_in['bq'], 'L0_xattn_Wk': _L0_xattn_in['Wk'], 'L0_xattn_bk': _L0_xattn_in['bk'], 'L0_xattn_Wv': _L0_xattn_in['Wv'], 'L0_xattn_bv': _L0_xattn_in['bv'], 'L0_xattn_Wo': _L0_xattn_in['Wo'], 'L0_xattn_bo': _L0_xattn_in['bo'], 'L0_ffn_cn_w1': _L0_ffn_in['cn_w1'], 'L0_ffn_cn_b1': _L0_ffn_in['cn_b1'], 'L0_ffn_cn_w2': _L0_ffn_in['cn_w2'], 'L0_ffn_cn_b2': _L0_ffn_in['cn_b2'], 'L0_ffn_cn_w3': _L0_ffn_in['cn_w3'], 'L0_ffn_cn_b3': _L0_ffn_in['cn_b3'], 'L0_ffn_cn_w4': _L0_ffn_in['cn_w4'], 'L0_ffn_cn_b4': _L0_ffn_in['cn_b4'], 'L0_ffn_gc_w1': _L0_ffn_in['gc_w1'], 'L0_ffn_gc_b1': _L0_ffn_in['gc_b1'], 'L0_ffn_gc_w2': _L0_ffn_in['gc_w2'], 'L0_ffn_gc_b2': _L0_ffn_in['gc_b2'], 'L0_ffn_gc_w3': _L0_ffn_in['gc_w3'], 'L0_ffn_gc_b3': _L0_ffn_in['gc_b3'], 'L0_ffn_adaptive_range': _L0_ffn_in['adaptive_range']}

def reference(x, ctx_1024, mask_Bx1xSxS2_ik1, g_xattn, g_ffn, L0_xattn_adj, L0_xattn_Wq, L0_xattn_bq, L0_xattn_Wk, L0_xattn_bk, L0_xattn_Wv, L0_xattn_bv, L0_xattn_Wo, L0_xattn_bo, L0_ffn_cn_w1, L0_ffn_cn_b1, L0_ffn_cn_w2, L0_ffn_cn_b2, L0_ffn_cn_w3, L0_ffn_cn_b3, L0_ffn_cn_w4, L0_ffn_cn_b4, L0_ffn_gc_w1, L0_ffn_gc_b1, L0_ffn_gc_w2, L0_ffn_gc_b2, L0_ffn_gc_w3, L0_ffn_gc_b3, L0_ffn_adaptive_range):
    import jax
    import jax.numpy as jnp

    def _L0_xattn_ref(query, key, value, adj, mask, Wq, bq, Wk, bk, Wv, bv, Wo, bo):
        import jax, jax.numpy as jnp
        import numpy as np
        B, S, E, H = (2, 1024, 512, 16)
        D = E // H
        b, s, _ = query.shape

        def heads(x, W, bias):
            y = jnp.einsum('bse,ef->bsf', x, W.T) + bias
            return y.reshape(b, s, H, D).transpose(0, 2, 1, 3)
        Q = heads(query, Wq, bq)
        K = heads(key, Wk, bk)
        V = heads(value, Wv, bv)
        scores = jnp.einsum('bhqd,bhkd->bhqk', Q, K) / jnp.sqrt(jnp.float32(D))
        scores = scores + adj[None, None, :, :]
        scores = jnp.where(mask == 0, jnp.float32(-jnp.inf), scores)
        weights = jax.nn.softmax(scores, axis=-1)
        out = jnp.einsum('bhqk,bhkd->bhqd', weights, V)
        out = out.transpose(0, 2, 1, 3).reshape(b, s, E)
        return jnp.einsum('bse,ef->bsf', out, Wo.T) + bo

    def _L0_ffn_ref(x, cn_w1, cn_b1, cn_w2, cn_b2, cn_w3, cn_b3, cn_w4, cn_b4, gc_w1, gc_b1, gc_w2, gc_b2, gc_w3, gc_b3, adaptive_range):
        import jax, jax.numpy as jnp
        import numpy as np
        B, S, DIM = (4, 2048, 512)
        BASE_COUPLING = 0.1
        NUM_CYCLES = 3

        def _gelu(x):
            return jax.nn.gelu(x, approximate=False)

        def _coupling_net(h, w1, b1, w2, b2, w3, b3, w4, b4):
            h = _gelu(h @ w1 + b1)
            h = _gelu(h @ w2 + b2)
            h = _gelu(h @ w3 + b3)
            return jax.nn.sigmoid(h @ w4 + b4)

        def _global_net(h, w1, b1, w2, b2, w3, b3):
            h = _gelu(h @ w1 + b1)
            h = _gelu(h @ w2 + b2)
            return jax.nn.sigmoid(h @ w3 + b3)

        def _twist(x):
            o_r, o_i, p_r, p_i = jnp.split(x, 4, axis=-1)
            return jnp.concatenate([p_r, -p_i, -o_r, o_i], axis=-1)
        global_context = x.mean(axis=1, keepdims=True)
        gf = _global_net(global_context, gc_w1, gc_b1, gc_w2, gc_b2, gc_w3, gc_b3)
        out = x
        for _ in range(NUM_CYCLES):
            tf = _coupling_net(out, cn_w1, cn_b1, cn_w2, cn_b2, cn_w3, cn_b3, cn_w4, cn_b4)
            combined = 0.7 * gf + 0.3 * tf
            coupling = BASE_COUPLING + adaptive_range * (combined - 0.5) * 2.0
            out = out + coupling * _twist(out)
        return out
    x = x + jnp.tanh(g_xattn[0]) * _L0_xattn_ref(_layernorm(x, axis=-1), ctx_1024, ctx_1024, L0_xattn_adj, mask_Bx1xSxS2_ik1, L0_xattn_Wq, L0_xattn_bq, L0_xattn_Wk, L0_xattn_bk, L0_xattn_Wv, L0_xattn_bv, L0_xattn_Wo, L0_xattn_bo)
    x = x + jnp.tanh(g_ffn[0]) * _L0_ffn_ref(_layernorm(x, axis=-1), L0_ffn_cn_w1, L0_ffn_cn_b1, L0_ffn_cn_w2, L0_ffn_cn_b2, L0_ffn_cn_w3, L0_ffn_cn_b3, L0_ffn_cn_w4, L0_ffn_cn_b4, L0_ffn_gc_w1, L0_ffn_gc_b1, L0_ffn_gc_w2, L0_ffn_gc_b2, L0_ffn_gc_w3, L0_ffn_gc_b3, L0_ffn_adaptive_range)
    return x

_drawn_inputs = setup_inputs


def setup_inputs(seed=0):
    import zlib

    import numpy as np

    out = dict(_drawn_inputs(seed))
    spreads = {'L0_ffn_cn_b1': (0.0, 0.8),
     'L0_ffn_cn_b2': (0.0, 0.8),
     'L0_ffn_cn_b3': (0.0, 0.8),
     'L0_ffn_gc_b1': (0.0, 0.75),
     'L0_ffn_gc_b2': (0.0, 0.769)}
    factors = {'L0_xattn_bq': 7.714, 'L0_xattn_bk': 8.0}
    for name, (base, spread) in spreads.items():
        noise = np.random.default_rng([zlib.crc32(name.encode()), seed]).standard_normal(out[name].shape)
        drawn = base * np.exp(spread * noise) if base else spread * noise
        out[name] = jnp.asarray(drawn.astype(out[name].dtype))
    for name, factor in factors.items():
        out[name] = (out[name] * factor).astype(out[name].dtype)
    return out
```

```python
from contextlib import ExitStack

import numpy as np

import concourse.bass as bass
from concourse import mybir

P = 128
F32 = mybir.dt.float32
F32R = mybir.dt.float32r
I32 = mybir.dt.int32
ALU = mybir.AluOpType
ACT = mybir.ActivationFunctionType

B, S, E, H = 4, 1024, 512, 16
D = E // H
TOK = B * S
ET = E // P
HPG = P // D
CH = 512
NCH = TOK // CH
TT = CH // P
EPS = 1e-5
BASE_COUPLING = 0.1
INV_SQRT_D = float(np.float32(1.0) / np.sqrt(np.float32(D)))
BIG = 3.0e38
ds = bass.ds


def wait(eng, sem, value):
    if isinstance(value, int) and value <= 0:
        return
    eng.wait_ge(sem, value)


def held_wait(eng, sem, value, passed):
    wait(eng, sem, value)
    if not isinstance(value, int):
        eng.sem_inc(passed, 1)


def make_identity(pool, ident, filled, ready):
    pool.memset(ident[:], 0.0).then_inc(filled, 1)
    pool.wait_ge(filled, 1)
    pool.affine_select(out=ident[:], in_=ident[:], compare_op=ALU.not_equal, fill=1.0,
                       base=0, pattern=[[-1, P]], channel_multiplier=1).then_inc(ready, 1)


def three_pass(pe, acc, w_hi, w_lo, r_hi, r_lo, first, last):
    pe.matmul(acc, w_hi, r_hi, start=first, stop=False)
    pe.matmul(acc, w_lo, r_hi, start=False, stop=False)
    return pe.matmul(acc, w_hi, r_lo, start=False, stop=last)


def project_phase(nc, x, ctxT, WqT, bq, WkT, bk, WvT, q_parts, k_parts, v_all):
    with ExitStack() as ctx:
        def sb(name, shape, dt=F32):
            return ctx.enter_context(nc.sbuf_tensor(name, shape, dt))

        def sem(name):
            return ctx.enter_context(nc.semaphore(name))

        w_raw = sb("p_w_raw", [P, 3, ET, E])
        w_hi = sb("p_w_hi", [P, 3, ET, E], F32R)
        w_lo = sb("p_w_lo", [P, 3, ET, E], F32R)
        x_raw = sb("p_x_raw", [P, TT, E])
        c_raw = sb("p_c_raw", [P, ET, CH])
        c_hi = sb("p_c_hi", [P, ET, CH], F32R)
        c_lo = sb("p_c_lo", [P, ET, CH], F32R)
        xn = sb("p_xn", [P, TT, E])
        xT_hi = sb("p_xT_hi", [P, ET, CH], F32R)
        xT_lo = sb("p_xT_lo", [P, ET, CH], F32R)
        k_hi = sb("p_k_hi", [P, ET, CH], F32R)
        k_lo = sb("p_k_lo", [P, ET, CH], F32R)
        q_hi = sb("p_q_hi", [P, ET, CH], F32R)
        q_lo = sb("p_q_lo", [P, ET, CH], F32R)
        v_out = sb("p_v_out", [P, TT, E])
        ident = sb("p_ident", [P, P])
        bias_q = sb("p_bias_q", [P, ET])
        bias_k = sb("p_bias_k", [P, ET])
        stats = sb("p_stats", [P, TT, 6])
        mv = sb("p_mv", [P, TT, 2])
        var_eps = sb("p_var_eps", [P, TT])
        rstd = sb("p_rstd", [P, TT])
        minus_half = sb("p_minus_half", [P, TT])
        acc = ctx.enter_context(nc.psum_tensor("p_acc", [P, 4, CH], F32))
        x_t = ctx.enter_context(nc.psum_tensor("p_x_t", [P, ET, CH], F32))

        w_loaded = [sem(f"p_w_loaded{n}") for n in range(3)]
        b_loaded = sem("p_b_loaded")
        x_loaded = sem("p_x_loaded")
        c_loaded = sem("p_c_loaded")
        id_filled = sem("p_id_filled")
        id_ready = sem("p_id_ready")
        bq_scaled = sem("p_bq_scaled")
        w_hi_ready = sem("p_w_hi_ready")
        w_lo_ready = sem("p_w_lo_ready")
        c_hi_ready = sem("p_c_hi_ready")
        c_lo_ready = sem("p_c_lo_ready")
        stats_ready = sem("p_stats_ready")
        mv_ready = sem("p_mv_ready")
        var_ready = sem("p_var_ready")
        rstd_ready = sem("p_rstd_ready")
        xn_ready = sem("p_xn_ready")
        xT_ready = sem("p_xT_ready")
        xT_hi_ready = sem("p_xT_hi_ready")
        xT_lo_ready = sem("p_xT_lo_ready")
        acc_ready = sem("p_acc_ready")
        acc_read = sem("p_acc_read")
        hi_ready = sem("p_hi_ready")
        q_done = sem("p_q_done")
        k_stored = sem("p_k_stored")
        v_stored = sem("p_v_stored")
        q_stored = sem("p_q_stored")
        pool_passed = sem("p_pool_passed")
        dve_passed = sem("p_dve_passed")

        block = ctx.enter_context(nc.Block())
        NACC = 3 * 4
        LOADS = ((WkT, 0), (WvT, 1), (WqT, 2))

        @block.gpsimd
        def _(pool):
            def load_weight(n):
                pool.dma_start(w_raw[:, n], LOADS[n][0].rearrange("(t p) f -> p t f", p=P)).then_inc(w_loaded[n], 16)

            pool.dma_start(c_raw[:], ctxT[0].rearrange("(t p) s -> p t s", p=P)).then_inc(c_loaded, 16)
            load_weight(0)
            pool.dma_start(x_raw[:], x[0:CH].rearrange("(t p) e -> p t e", p=P)).then_inc(x_loaded, 16)
            load_weight(1)
            load_weight(2)
            make_identity(pool, ident, id_filled, id_ready)
            pool.memset(minus_half[:], -0.5).then_inc(id_filled, 1)
            pool.wait_ge(id_filled, 2)

            def inverse_std(c):
                held_wait(pool, mv_ready, c + 1, pool_passed)
                pool.tensor_scalar(var_eps[:], mv[:, :, 1], EPS, 1.0, ALU.add, ALU.mult).then_inc(var_ready, 1)
                pool.wait_ge(var_ready, c + 1)
                pool.tensor_tensor(rstd[:], var_eps[:], minus_half[:], ALU.pow).then_inc(rstd_ready, 1)

            inverse_std(0)
            with pool.Fori(1, NCH) as c:
                pool.wait_ge(xn_ready, c)
                pool.dma_start(x_raw[:], x[ds(c * CH, CH), :].rearrange("(t p) e -> p t e", p=P)).then_inc(x_loaded, 16)
                pool.wait_ge(c_lo_ready, c)
                pool.dma_start(c_raw[:], ctxT[ds(c, 1)].rearrange("a (t p) s -> p (a t) s", p=P)).then_inc(c_loaded, 16)
                inverse_std(c)

        @block.sync
        def _(sp):
            with nc.allow_non_contiguous_dma(reason="a bias of one element per partition"):
                sp.dma_start(bias_q[:], bq.rearrange("(t p) -> p t", p=P)).then_inc(b_loaded, 16)
                sp.dma_start(bias_k[:], bk.rearrange("(t p) -> p t", p=P)).then_inc(b_loaded, 16)

            def store_parts(parts, tile, part, col, stored):
                sp.dma_start(parts[part].rearrange("(t p) s -> p t s", p=P)[:, :, ds(col, CH)],
                             tile[:].bitcast(F32)).then_inc(stored, 16)

            with sp.Fori(0, NCH) as c:
                sp.wait_ge(hi_ready, 8 * c + 4)
                store_parts(k_parts, k_hi, 0, c * CH, k_stored)
                sp.wait_ge(acc_read, NACC * c + 4 + 4)
                store_parts(k_parts, k_lo, 1, c * CH, k_stored)
                sp.wait_ge(acc_read, NACC * c + 8 + 4)
                sp.dma_start(v_all[ds(c * CH, CH), :].rearrange("(t p) f -> p t f", p=P), v_out[:]).then_inc(v_stored, 16)
                sp.wait_ge(hi_ready, 8 * c + 8)
                store_parts(q_parts, q_hi, 0, c * CH, q_stored)
                sp.wait_ge(acc_read, NACC * c + 12 + 4)
                store_parts(q_parts, q_lo, 1, c * CH, q_stored)
            sp.wait_ge(k_stored, 32 * NCH)
            sp.wait_ge(v_stored, 16 * NCH)
            sp.wait_ge(q_stored, 32 * NCH)

        @block.tensor
        def _(pe):
            def product(c, n, lhs, rhs):
                pe.wait_ge(acc_read, NACC * c + n + 1)
                for t in range(ET):
                    last = three_pass(pe, acc[:, n % 4, :], lhs(0, t), lhs(1, t), rhs(0, t), rhs(1, t), t == 0, t == ET - 1)
                return last

            pe.wait_ge(id_ready, 1)

            def chunk(c, first):
                pe.wait_ge(xn_ready, c + 1)
                for t in range(ET):
                    for s in range(TT):
                        last = pe.transpose(x_t[:, t, s * P:(s + 1) * P], xn[:, s, t * P:(t + 1) * P], ident[:])
                    last.then_inc(xT_ready, 1)
                if first:
                    pe.wait_ge(w_hi_ready, 1)
                    pe.wait_ge(w_lo_ready, 1)
                pe.wait_ge(c_hi_ready, c + 1)
                pe.wait_ge(c_lo_ready, c + 1)
                cs = (c_hi, c_lo)
                xs = (xT_hi, xT_lo)
                for m in range(4):
                    w = lambda part, t: (w_hi, w_lo)[part][:, 0, t, m * P:(m + 1) * P]
                    product(c, m, w, lambda part, t: cs[part][:, t, :]).then_inc(acc_ready, 1)
                if first:
                    pe.wait_ge(w_hi_ready, 2)
                    pe.wait_ge(w_lo_ready, 2)
                for m in range(4):
                    w = lambda part, t: cs[part][:, t, m * P:(m + 1) * P]
                    product(c, 4 + m, w, lambda part, t: (w_hi, w_lo)[part][:, 1, t, :]).then_inc(acc_ready, 1)
                if first:
                    pe.wait_ge(w_hi_ready, 3)
                    pe.wait_ge(w_lo_ready, 3)
                pe.wait_ge(xT_hi_ready, 4 * c + 4)
                pe.wait_ge(xT_lo_ready, 4 * c + 4)
                for m in range(4):
                    w = lambda part, t: (w_hi, w_lo)[part][:, 2, t, m * P:(m + 1) * P]
                    product(c, 8 + m, w, lambda part, t: xs[part][:, t, :]).then_inc(acc_ready, 1)

            chunk(0, True)
            with pe.Fori(1, NCH) as c:
                chunk(c, False)

        @block.scalar
        def _(act):
            def split_context(c):
                act.wait_ge(c_loaded, 16 * (c + 1))
                wait(act, acc_ready, NACC * c - 4)
                act.activation(c_hi[:], c_raw[:], ACT.Copy).then_inc(c_hi_ready, 1)

            def split_weight(n):
                act.wait_ge(w_loaded[n], 16)
                act.activation(w_hi[:, n], w_raw[:, n], ACT.Copy, scale=INV_SQRT_D if n == 2 else 1.0).then_inc(w_hi_ready, 1)

            split_context(0)
            split_weight(0)
            split_weight(1)
            split_weight(2)
            act.wait_ge(b_loaded, 32)
            act.wait_ge(bq_scaled, 1)

            def high_parts(c, n0, out, bias, stored):
                wait(act, stored, 32 * c)
                for m in range(4):
                    act.wait_ge(acc_ready, NACC * c + n0 + m + 1)
                    act.activation(out[:, m, :], acc[:, (n0 + m) % 4, :], ACT.Identity,
                                   bias=bias[:, m:m + 1]).then_inc(hi_ready, 1)

            def chunk(c, more):
                for t in range(ET):
                    act.wait_ge(xT_ready, 4 * c + t + 1)
                    wait(act, acc_ready, NACC * c)
                    act.activation(xT_hi[:, t, :], x_t[:, t, :], ACT.Copy).then_inc(xT_hi_ready, 1)
                high_parts(c, 0, k_hi, bias_k, k_stored)
                if more:
                    split_context(c + 1)
                high_parts(c, 8, q_hi, bias_q, q_stored)

            chunk(0, True)
            with act.Fori(1, NCH - 1) as c:
                chunk(c, True)
            chunk(NCH - 1, False)

        @block.vector
        def _(dve):
            dve.sem_inc(acc_read, 4)

            def norm_stats(c):
                dve.wait_ge(x_loaded, 16 * (c + 1))
                for s in range(TT):
                    last = dve.bn_stats(stats[:, s, :], x_raw[:, s, :])
                last.then_inc(stats_ready, 1)
                held_wait(dve, stats_ready, c + 1, dve_passed)
                for s in range(TT):
                    last = dve.bn_aggr(mv[:, s, :], stats[:, s, :])
                last.then_inc(mv_ready, 1)

            def norm_apply(c):
                dve.wait_ge(rstd_ready, c + 1)
                wait(dve, xT_ready, 4 * c)
                dve.wait_ge(mv_ready, c + 1)
                for s in range(TT):
                    last = dve.tensor_scalar(xn[:, s, :], x_raw[:, s, :], mv[:, s, 0:1], rstd[:, s:s + 1], ALU.subtract, ALU.mult)
                last.then_inc(xn_ready, 1)

            def split_context(c):
                dve.wait_ge(c_hi_ready, c + 1)
                dve.tensor_tensor(c_lo[:], c_raw[:], c_hi[:].bitcast(F32), ALU.subtract).then_inc(c_lo_ready, 1)

            def split_weight(n):
                dve.wait_ge(w_hi_ready, n + 1)
                dve.scalar_tensor_tensor(w_lo[:, n], w_raw[:, n], INV_SQRT_D if n == 2 else 1.0, w_hi[:, n].bitcast(F32),
                                         ALU.mult, ALU.subtract).then_inc(w_lo_ready, 1)

            norm_stats(0)
            split_context(0)
            split_weight(0)
            norm_apply(0)
            split_weight(1)
            split_weight(2)
            dve.wait_ge(b_loaded, 32)
            dve.tensor_scalar(bias_q[:], bias_q[:], INV_SQRT_D, None, ALU.mult).then_inc(bq_scaled, 1)
            dve.wait_ge(bq_scaled, 1)

            def low_parts(c, n0, h0, out, high, bias, stored):
                wait(dve, stored, 32 * c)
                for m in range(4):
                    dve.wait_ge(hi_ready, 8 * c + h0 + m + 1)
                    dve.scalar_tensor_tensor(out[:, m, :], acc[:, (n0 + m) % 4, :], bias[:, m:m + 1],
                                             high[:, m, :].bitcast(F32), ALU.add, ALU.subtract).then_inc(acc_read, 1)

            def chunk(c, more):
                for t in range(ET):
                    dve.wait_ge(xT_hi_ready, 4 * c + t + 1)
                    dve.tensor_tensor(xT_lo[:, t, :], x_t[:, t, :], xT_hi[:, t, :].bitcast(F32), ALU.subtract).then_inc(xT_lo_ready, 1)
                low_parts(c, 0, 0, k_lo, k_hi, bias_k, k_stored)
                wait(dve, v_stored, 16 * c)
                for m in range(4):
                    dve.wait_ge(acc_ready, NACC * c + 4 + m + 1)
                    dve.tensor_copy(v_out[:, m, :], acc[:, m, :]).then_inc(acc_read, 1)
                if more:
                    norm_stats(c + 1)
                    split_context(c + 1)
                    norm_apply(c + 1)
                low_parts(c, 8, 4, q_lo, q_hi, bias_q, q_stored)

            chunk(0, True)
            with dve.Fori(1, NCH - 1) as c:
                chunk(c, True)
            chunk(NCH - 1, False)


def attention_phase(nc, adj, mask, q_parts, k_parts, v_all, o_all, rinv_all):
    QB = 256
    NQB = S // QB
    UB = HPG * QB // P
    UG = UB * NQB
    NG = B * H // HPG
    NU = NG * UG
    PAIR = 2 * UG
    NPAIR = NU // PAIR
    LEAD = 2 * UB
    GPB = H // HPG
    BPB = GPB * NQB
    KT = S // P
    NPROB = 4
    AHEAD = 3
    ACT_LAG, DVE_LAG = 2, 3
    STACK = 3 * D

    with ExitStack() as ctx:
        def sb(name, shape, dt=F32):
            return ctx.enter_context(nc.sbuf_tensor(name, shape, dt))

        def sem(name):
            return ctx.enter_context(nc.semaphore(name))

        q_st = sb("a_q_st", [P, NQB, HPG, QB], F32R)
        k_st = sb("a_k_st", [P, 2, HPG, S], F32R)
        v_sb = sb("a_v", [P, 2, KT, P])
        am = sb("a_am", [P, KT, S])
        neg = sb("a_neg", [P, 2, S])
        prob = sb("a_prob", [P, NPROB, S])
        probT = sb("a_probT", [P, 2, HPG, KT, QB])
        o_sb = sb("a_o", [P, 2, QB])
        m_raw = sb("a_m_raw", [P, S], I32)
        adj_raw = sb("a_adj_raw", [P, S])
        m_big = sb("a_m_big", [P, S])
        row_min = sb("a_row_min", [P, 2])
        row_sum = sb("a_row_sum", [P, 2, UG])
        rinv = sb("a_rinv", [P, P])
        rinvT = sb("a_rinvT", [UG, P])
        ident = sb("a_ident", [P, P])
        sc_ps = ctx.enter_context(nc.psum_tensor("a_sc_ps", [P, 2, S], F32))
        tr_ps = ctx.enter_context(nc.psum_tensor("a_tr_ps", [P, 2, 4 * P], F32))
        o_ps = ctx.enter_context(nc.psum_tensor("a_o_ps", [P, 2, 512], F32))

        q_loaded = [sem(f"a_q_loaded{n}") for n in range(NQB)]
        k_loaded = [sem(f"a_k_loaded{n}") for n in range(2)]
        v_loaded = [sem(f"a_v_loaded{n}") for n in range(2)]
        adj_loaded = sem("a_adj_loaded")
        m_loaded = sem("a_m_loaded")
        id_filled = sem("a_id_filled")
        id_ready = sem("a_id_ready")
        rinv_filled = sem("a_rinv_filled")
        big_ready = sem("a_big_ready")
        am_ready = sem("a_am_ready")
        am_built = sem("a_am_built")
        sc_ready = sem("a_sc_ready")
        neg_ready = sem("a_neg_ready")
        prob_ready = sem("a_prob_ready")
        tr_ready = [sem(f"a_tr_ready{n}") for n in range(2)]
        tr_read = [sem(f"a_tr_read{n}") for n in range(2)]
        pv_ready = sem("a_pv_ready")
        o_ready = sem("a_o_ready")
        rinv_ready = sem("a_rinv_ready")
        rinvT_ps_ready = sem("a_rinvT_ps_ready")
        rinvT_ready = sem("a_rinvT_ready")
        o_stored = [sem(f"a_o_stored{n}") for n in range(2)]
        rinv_stored = sem("a_rinv_stored")
        pool_passed = sem("a_pool_passed")
        dve_passed = sem("a_dve_passed")
        sp_passed = sem("a_sp_passed")

        block = ctx.enter_context(nc.Block())

        def run(eng, step):
            for r in range(LEAD):
                step(0, r)
            with eng.Fori(0, NPAIR - 1) as i:
                for v in range(LEAD, LEAD + PAIR):
                    step(i + v // PAIR, v % PAIR)
            for r in range(LEAD, PAIR):
                step(NPAIR - 1, r)

        def shifted(p, r, k):
            return p + (r + k) // PAIR, (r + k) % PAIR

        def exists(p, r):
            return not (isinstance(p, int) and (PAIR * p + r < 0 or PAIR * p + r >= NU))

        def parts(p, r):
            return PAIR * p + r, (PAIR // UB) * p + r // UB, 2 * p + r // UG

        @block.sync
        def _(sp):
            for n in range(2):
                sp.sem_inc(o_stored[n], 16)
            sp.sem_inc(rinv_stored, 16)

            def load_v(b, g):
                G = GPB * b + g
                held_wait(sp, pv_ready, NQB * (G - 1), sp_passed)
                sp.dma_start(v_sb[:, g % 2], v_all[ds(b * S, S), g * P:(g + 1) * P].rearrange("(t p) f -> p t f", p=P)
                             ).then_inc(v_loaded[g % 2], 16)

            def store_o(b, g, qb, first):
                k = NQB * g + qb - 2
                if first and k < 0:
                    return
                bb, k = (b, k) if k >= 0 else (b - 1, k + BPB)
                gg, qq = k // NQB, k % NQB
                n = BPB * bb + k
                held_wait(sp, o_ready, n + 2, sp_passed)
                sp.dma_start(o_all[gg * P:(gg + 1) * P, ds(bb * S + qq * QB, QB)], o_sb[:, k % 2]).then_inc(o_stored[k % 2], 16)

            def store_rinv(G):
                sp.wait_ge(rinvT_ready, G + 1)
                sp.dma_start(rinv_all[ds(G, 1)].rearrange("a r s -> (a r) s"), rinvT[:]).then_inc(rinv_stored, 16)

            def batch(b, first):
                for g in range(GPB):
                    load_v(b, g)
                    for qb in range(NQB):
                        if not (first and g == 0):
                            gg, bb = (g - 1, b) if g else (GPB - 1, b - 1)
                            store_o(bb, gg, qb, first and g == 1)
                            if qb == NQB - 1 and not (first and g == 1):
                                store_rinv(GPB * bb + gg - 1)

            batch(0, True)
            with sp.Fori(1, B) as b:
                batch(b, False)
            for qb in range(NQB):
                store_o(B - 1, GPB - 1, qb, False)
            store_rinv(NG - 2)
            store_o(B, 0, 0, False)
            store_o(B, 0, 1, False)
            store_rinv(NG - 1)
            for n in range(2):
                sp.wait_ge(o_stored[n], 16 * NG * NQB // 2 + 16)
            sp.wait_ge(rinv_stored, 16 * (NG + 1))

        @block.gpsimd
        def _(pool):
            make_identity(pool, ident, id_filled, id_ready)

            def load_k(b, g):
                G = GPB * b + g
                held_wait(pool, sc_ready, UG * (G - 1), pool_passed)
                for quad, part in enumerate((0, 1, 0)):
                    src = k_parts[part, g * P:(g + 1) * P, ds(b * S, S)].rearrange("(h d) s -> d h s", d=D)
                    pool.dma_start(k_st[quad * D:(quad + 1) * D, g % 2], src).then_inc(k_loaded[g % 2], 16)

            def load_q(b, g, qb):
                G = GPB * b + g
                held_wait(pool, sc_ready, UG * (G - 1) + UB * (qb + 1), pool_passed)
                for quad, part in enumerate((0, 0, 1)):
                    src = q_parts[part, g * P:(g + 1) * P, ds(b * S + qb * QB, QB)].rearrange("(h d) s -> d h s", d=D)
                    pool.dma_start(q_st[quad * D:(quad + 1) * D, qb], src).then_inc(q_loaded[qb], 16)

            def mask_tile(b, t, first):
                n = KT * b + t
                held_wait(pool, big_ready, n, pool_passed)
                pool.dma_start(m_raw[:], mask[ds(b * S + t * P, P), :]).then_inc(m_loaded, 16)
                held_wait(pool, am_built, n, pool_passed)
                pool.dma_start(adj_raw[:], adj[t * P:(t + 1) * P, :]).then_inc(adj_loaded, 16)
                held_wait(pool, m_loaded, 16 * (n + 1), pool_passed)
                pool.tensor_scalar(m_big[:], m_raw[:], 0.0, -BIG, ALU.is_equal, ALU.mult).then_inc(big_ready, 1)
                pool.wait_ge(big_ready, n + 1)
                pool.wait_ge(adj_loaded, 16 * (n + 1))
                if not first:
                    pool.wait_ge(neg_ready, (GPB * b - 1) * UG + UB * (t // 2 + 1))
                pool.tensor_tensor(am[:, t, :], m_big[:], adj_raw[:], ALU.add).then_inc(am_built, 1)

            def batch(b, first):
                for g in range(GPB):
                    load_k(b, g)
                    for qb in range(NQB):
                        load_q(b, g, qb)
                        if g == 0:
                            mask_tile(b, 2 * qb, first)
                            mask_tile(b, 2 * qb + 1, first)
                            pool.wait_ge(am_built, KT * b + 2 * qb + 2)
                            pool.sem_inc(am_ready, 1)
                    if g == 0:
                        pool.sem_inc(am_ready, BPB - NQB)

            batch(0, True)
            with pool.Fori(1, B) as b:
                batch(b, False)

        @block.tensor
        def _(pe):
            pe.sem_inc(rinvT_ps_ready, 1)
            pe.wait_ge(id_ready, 1)

            def scores(p, r):
                if not exists(p, r):
                    return
                u, blk, G = parts(p, r)
                par, qb, h, qt = r // UG, (r // UB) % NQB, r % UB // 2, r % 2
                if r % UG == 0:
                    pe.wait_ge(k_loaded[par], 48 * (p + 1))
                if r % UB == 0:
                    pe.wait_ge(q_loaded[qb], 48 * (2 * p + par + 1))
                wait(pe, neg_ready, u - 1)
                for half in range(2):
                    last = pe.matmul(sc_ps[:, r % 2, half * 512:(half + 1) * 512],
                                     q_st[0:STACK, qb, h, qt * P:(qt + 1) * P],
                                     k_st[0:STACK, par, h, half * 512:(half + 1) * 512], start=True, stop=True)
                last.then_inc(sc_ready, 1)

            def transposes(p, r, half):
                u, _, _ = parts(p, r)
                if half == 0:
                    pe.wait_ge(prob_ready, u + 1)
                wait(pe, tr_read[half], u)
                for j in range(4):
                    t = 4 * half + j
                    last = pe.transpose(tr_ps[:, half, j * P:(j + 1) * P], prob[:, r % NPROB, t * P:(t + 1) * P], ident[:])
                last.then_inc(tr_ready[half], 1)

            def weighted_values(p, r):
                u, blk, _ = parts(p, r)
                t = r % UB
                prev = r // UB - 1
                if isinstance(p, int) and p == 0 and prev < 0:
                    return
                vpar = (prev // NQB) % 2 if prev >= 0 else 1
                if t % 4 == 0:
                    pe.wait_ge(tr_read[t // 4], UB * blk)
                if t == 0:
                    wait(pe, o_ready, blk - 1)
                    if prev % NQB == 0:
                        pe.wait_ge(v_loaded[vpar], 16 * (p + 1))
                    if r == UB or r == UB + UG:
                        wait(pe, rinvT_ready, 2 * p + r // UG)
                for h in range(HPG):
                    last = pe.matmul(o_ps[h * D:(h + 1) * D, prev % 2, 0:QB], v_sb[:, vpar, t, h * D:(h + 1) * D],
                                     probT[:, prev % 2, h, t, :], start=(t == 0), stop=(t == KT - 1))
                if t == KT - 1:
                    last.then_inc(pv_ready, 1)

            def transpose_rinv(G, first):
                if first:
                    return
                pe.wait_ge(rinv_ready, G)
                pe.wait_ge(o_ready, NQB * G)
                pe.transpose(o_ps[:, 0, QB:QB + P], rinv[:], ident[:]).then_inc(rinvT_ps_ready, 1)

            def step(p, r):
                transposes(p, r, 0)
                scores(*shifted(p, r, AHEAD))
                transposes(p, r, 1)
                weighted_values(p, r)
                if r % UG == 3:
                    transpose_rinv(2 * p + r // UG, isinstance(p, int) and p == 0 and r < UG)

            for r in range(AHEAD):
                scores(0, r)
            run(pe, step)
            for r in range(UB):
                weighted_values(NPAIR, r)
            transpose_rinv(NG, False)

        @block.scalar
        def _(act):
            def read_transposes(p, r):
                if not exists(p, r):
                    return
                u, _, _ = parts(p, r)
                h, qt = r % UB // 2, r % 2
                act.wait_ge(tr_ready[0], u + 1)
                if r % UB == 0:
                    wait(act, pv_ready, (PAIR // UB) * p + r // UB - 1)
                act.activation(probT[:, (r // UB) % 2, h, 0:4, qt * P:(qt + 1) * P],
                               tr_ps[:, 0, :].rearrange("p (t q) -> p t q", t=4), ACT.Copy).then_inc(tr_read[0], 1)

            def step(p, r):
                u, _, _ = parts(p, r)
                qb, h, qt = (r // UB) % NQB, r % UB // 2, r % 2
                col = h * KT + 2 * qb + qt
                act.wait_ge(neg_ready, u + 1)
                for half in range(2):
                    wait(act, tr_ready[half], u - NPROB + 1)
                act.activation(prob[:, r % NPROB, :], neg[:, r % 2, :], ACT.Exp, scale=-1.0, bias=row_min[:, r % 2:r % 2 + 1],
                               accum_out=row_sum[:, r // UG, col:col + 1]).then_inc(prob_ready, 1)
                read_transposes(*shifted(p, r, -ACT_LAG))

            run(act, step)
            for k in range(ACT_LAG, 0, -1):
                read_transposes(NPAIR - 1, PAIR - k)

        @block.vector
        def _(dve):
            dve.sem_inc(o_ready, 1)
            dve.memset(rinv[:], 1.0).then_inc(rinv_filled, 1)
            dve.wait_ge(rinv_filled, 1)

            def read_transposes(p, r):
                if not exists(p, r):
                    return
                u, _, _ = parts(p, r)
                h, qt = r % UB // 2, r % 2
                if r % UB == 0:
                    wait(dve, pv_ready, (PAIR // UB) * p + r // UB - 1)
                dve.wait_ge(tr_ready[1], u + 1)
                dve.tensor_copy(probT[:, (r // UB) % 2, h, 4:8, qt * P:(qt + 1) * P],
                                tr_ps[:, 1, :].rearrange("p (t q) -> p t q", t=4)).then_inc(tr_read[1], 1)

            def read_output(blk, par, first):
                if first:
                    return
                dve.wait_ge(pv_ready, blk + 1)
                dve.wait_ge(o_stored[par], 8 * (blk - par) + 16)
                dve.tensor_copy(o_sb[:, par, :], o_ps[:, par, 0:QB]).then_inc(o_ready, 1)

            def inverse_sums(G, par, first):
                if first:
                    return
                dve.wait_ge(prob_ready, UG * G)
                wait(dve, rinvT_ps_ready, G)
                dve.reciprocal(rinv[:, 0:UG], row_sum[:, par, :]).then_inc(rinv_ready, 1)

            def read_rinv(G, first):
                if first:
                    return
                dve.wait_ge(rinvT_ps_ready, G + 1)
                dve.wait_ge(rinv_stored, 16 * G)
                dve.tensor_copy(rinvT[:], o_ps[0:UG, 0, QB:QB + P]).then_inc(rinvT_ready, 1)

            def step(p, r):
                u, blk, G = parts(p, r)
                qb, qt = (r // UB) % NQB, r % 2
                first = isinstance(p, int) and p == 0
                if r % UB == 0:
                    dve.wait_ge(am_ready, blk + 1)
                wait(dve, prob_ready, u - 1)
                held_wait(dve, sc_ready, u + 1, dve_passed)
                dve.tensor_tensor_reduce(out=neg[:, r % 2, :], in0=sc_ps[:, r % 2, :], in1=am[:, 2 * qb + qt, :],
                                         scale=-1.0, scalar=3.4e38, op0=ALU.add, op1=ALU.min,
                                         accum_out=row_min[:, r % 2:r % 2 + 1]).then_inc(neg_ready, 1)
                read_transposes(*shifted(p, r, -DVE_LAG))
                if r % UB == 5:
                    read_output(blk - 2, (r // UB) % 2, first and r // UB < 2)
                if r % UG == 3:
                    inverse_sums(G, 1 - r // UG, first and r < UG)
                if r % UG == 7:
                    read_rinv(G, first and r < UG)

            run(dve, step)
            for k in range(DVE_LAG, 0, -1):
                read_transposes(NPAIR - 1, PAIR - k)
            read_output(NU // UB - 2, 0, False)
            inverse_sums(NG, 1, False)
            read_output(NU // UB - 1, 1, False)
            read_rinv(NG, False)


def ffn_phase(nc, x, o_all, rinv_all, g_xattn, g_ffn, bv, WoT, bo, cn_w1, cn_b1, cn_w2, cn_b2, cn_w3, cn_b3, cn_w4, cn_b4,
              gc_w1, gc_b1, gc_w2, gc_b2, gc_w3, gc_b3, adaptive_range, out):
    NJ = S // CH
    F2, F3 = E // 2, E // 4
    CYCLES = 3
    GPB = H // HPG
    TWIST = ((2, -1), (3, 1), (0, 1), (1, -1))

    with ExitStack() as ctx:
        def sb(name, shape, dt=F32):
            return ctx.enter_context(nc.sbuf_tensor(name, shape, dt))

        def ps(name, shape):
            return ctx.enter_context(nc.psum_tensor(name, shape, F32))

        def sem(name):
            return ctx.enter_context(nc.semaphore(name))

        wo_hi = sb("f_wo_hi", [P, ET, E], F32R)
        wo_lo = sb("f_wo_lo", [P, ET, E], F32R)
        w1_hi = sb("f_w1_hi", [P, ET, E], F32R)
        w1_lo = sb("f_w1_lo", [P, ET, E], F32R)
        neg_hi = sb("f_neg_hi", [P, 2, E], F32R)
        neg_lo = sb("f_neg_lo", [P, 2, E], F32R)
        w2 = sb("f_w2", [P, ET, F2])
        w3 = sb("f_w3", [P, 2, F3])
        w4_col = sb("f_w4_col", [P, 1])
        w4 = sb("f_w4", [P, P])
        gw1 = sb("f_gw1", [P, ET, F2])
        gw2 = sb("f_gw2", [P, 2, F3])
        gw3_col = sb("f_gw3_col", [P, 1])
        gw3 = sb("f_gw3", [P, P])
        b1 = sb("f_b1", [P, ET])
        b2 = sb("f_b2", [P, 2])
        b3 = sb("f_b3", [P, 1])
        half_b4 = sb("f_half_b4", [P, 1])
        gb1 = sb("f_gb1", [P, 2])
        gb2 = sb("f_gb2", [P, 1])
        half_gb3 = sb("f_half_gb3", [P, 1])
        bv_sb = sb("f_bv", [P, ET])
        gate_x = sb("f_gate_x", [P, 1])
        gate_f = sb("f_gate_f", [P, 1])
        range_3 = sb("f_range_3", [P, 1])
        range_7 = sb("f_range_7", [P, 1])
        gated_bo = sb("f_gated_bo", [P, E])
        ident = sb("f_ident", [P, P])

        X_hi = [sb(f"f_X_hi{j}", [P, ET, CH], F32R) for j in range(NJ)]
        X_lo = [sb(f"f_X_lo{j}", [P, ET, CH], F32R) for j in range(NJ)]
        o_raw = sb("f_o_raw", [P, ET, CH])
        rinv = sb("f_rinv", [P, ET, CH])
        x_pre = (o_raw, rinv)
        x1 = [sb(f"f_x1_{j}", [P, TT, E]) for j in range(NJ)]
        xn = [sb(f"f_xn{j}", [P, TT, E]) for j in range(NJ)]
        A = [sb(f"f_A{j}", [P, ET, CH]) for j in range(NJ)]
        Bt = [sb(f"f_B{j}", [P, ET, CH]) for j in range(NJ)]
        u = [sb(f"f_u{j}", [P, ET, CH]) for j in range(NJ)]
        h2 = [sb(f"f_h2_{j}", [P, 2, CH]) for j in range(NJ)]
        coef = sb("f_coef", [P, NJ, CH])
        alpha = sb("f_alpha", [P, NJ, CH])
        beta = sb("f_beta", [P, NJ, CH])
        cross = sb("f_cross", [P, CH])
        stats = sb("f_stats", [P, TT, 6])
        mv = sb("f_mv", [P, TT, 2])
        var_eps = sb("f_var_eps", [P, TT])
        rstd = sb("f_rstd", [P, TT])
        minus_half = sb("f_minus_half", [P, TT])
        sums = sb("f_sums", [P, NJ, ET])
        total = sb("f_total", [P, ET])
        g1 = sb("f_g1", [P, 2])
        g2 = sb("f_g2", [P, 1])
        g_tanh = sb("f_g_tanh", [P, 1])
        base = sb("f_base", [P, 1])
        cols = sb("f_cols", [P, NJ, 2 * TT])
        neg_cols = sb("f_neg_cols", [P, NJ, TT])

        acc = ps("f_acc", [P, 4, CH])
        tr = ps("f_tr", [P, 2, CH])
        z4 = ps("f_z4", [P, NJ, CH])

        small_loaded = sem("f_small_loaded")
        bv_loaded = sem("f_bv_loaded")
        wo_loaded = sem("f_wo_loaded")
        w1_loaded = sem("f_w1_loaded")
        w_loaded = sem("f_w_loaded")
        o_loaded = [sem(f"f_o_loaded{j}") for j in range(NJ)]
        rinv_loaded = [sem(f"f_rinv_loaded{j}") for j in range(NJ)]
        x_loaded = [sem(f"f_x_loaded{j}") for j in range(NJ)]
        y_stored = [sem(f"f_y_stored{j}") for j in range(NJ)]
        id_filled = sem("f_id_filled")
        id_ready = sem("f_id_ready")
        gates_ready = sem("f_gates_ready")
        scaled = sem("f_scaled")
        copied = sem("f_copied")
        wo_hi_ready = sem("f_wo_hi_ready")
        wo_lo_ready = sem("f_wo_lo_ready")
        w1_hi_ready = sem("f_w1_hi_ready")
        w1_lo_ready = sem("f_w1_lo_ready")
        neg_ready = sem("f_neg_ready")
        att_ready = sem("f_att_ready")
        att_hi_ready = sem("f_att_hi_ready")
        att_lo_ready = sem("f_att_lo_ready")
        o_ready = sem("f_o_ready")
        xbo_ready = sem("f_xbo_ready")
        x1_ready = sem("f_x1_ready")
        stats_ready = sem("f_stats_ready")
        mv_ready = sem("f_mv_ready")
        var_ready = sem("f_var_ready")
        rstd_ready = sem("f_rstd_ready")
        xn_ready = sem("f_xn_ready")
        xT_ready = sem("f_xT_ready")
        xT_hi_ready = sem("f_xT_hi_ready")
        xT_lo_ready = sem("f_xT_lo_ready")
        A_ready = sem("f_A_ready")
        B_ready = sem("f_B_ready")
        A_read = sem("f_A_read")
        B_read = sem("f_B_read")
        total_ready = sem("f_total_ready")
        gz1_ready = sem("f_gz1_ready")
        g1_ready = sem("f_g1_ready")
        gz2_ready = sem("f_gz2_ready")
        g2_ready = sem("f_g2_ready")
        gz3_ready = sem("f_gz3_ready")
        g3_ready = sem("f_g3_ready")
        base_ready = sem("f_base_ready")
        mul_ready = sem("f_mul_ready")
        B_scaled = sem("f_B_scaled")
        u_ready = sem("f_u_ready")
        h1_ready = sem("f_h1_ready")
        z2_ready = sem("f_z2_ready")
        h2_ready = sem("f_h2_ready")
        z3_ready = sem("f_z3_ready")
        h3_ready = sem("f_h3_ready")
        z4_ready = sem("f_z4_ready")
        t_ready = sem("f_t_ready")
        coef_step = sem("f_coef_step")
        cols_ps_ready = sem("f_cols_ps_ready")
        cols_ready = sem("f_cols_ready")
        y_base = sem("f_y_base")
        y_ready = sem("f_y_ready")
        pool_passed = sem("f_pool_passed")
        dve_passed = sem("f_dve_passed")
        block = ctx.enter_context(nc.Block())

        def turn(b, n, j):
            return (CYCLES * b + n) * NJ + j

        def coef_steps(b, n, j):
            per_cycle = (1, 4, 5)
            return NJ * sum(per_cycle) * b + NJ * sum(per_cycle[:n]) + per_cycle[n] * (j + 1)

        def batches(eng, body):
            body(0, True, True)
            with eng.Fori(1, B - 1) as b:
                body(b, False, True)
            body(B - 1, False, False)

        def rows(array, b, j):
            return array[ds(b * S + j * CH, CH), :].rearrange("(t p) e -> p t e", p=P)

        @block.sync
        def _(sp):
            def load_weighted(b, j, tile):
                sp.dma_start(tile[:], o_all.rearrange("(t p) s -> p t s", p=P)[:, :, ds(b * S + j * CH, CH)]).then_inc(o_loaded[j], 16)

            def load_rinv(b, j, tile):
                for h in range(HPG):
                    row = h * (S // P) + j * TT
                    sp.dma_start(tile[h * D:(h + 1) * D], rinv_all[ds(b * GPB, GPB), row:row + TT, :].rearrange(
                        "t q s -> t (q s)").partition_broadcast(D)).then_inc(rinv_loaded[j], 16)

            def load_x(b, j):
                sp.wait_ge(att_ready if j == 0 else att_lo_ready, NJ * b + NJ)
                sp.dma_start(x_pre[j][:], rows(x, b, j)).then_inc(x_loaded[j], 16)

            def store_y(b, j):
                sp.wait_ge(y_ready, NJ * b + j + 1)
                sp.dma_start(rows(out, b, j), u[j][:]).then_inc(y_stored[j], 16)

            load_weighted(0, 0, o_raw)
            load_rinv(0, 0, rinv)
            load_weighted(0, 1, Bt[0])
            load_rinv(0, 1, Bt[1])
            for tile, array in ((w2, cn_w2), (w3, cn_w3), (gw1, gc_w1), (gw2, gc_w2)):
                sp.dma_start(tile[:], array.rearrange("(t p) f -> p t f", p=P)).then_inc(w_loaded, 16)
            load_x(0, 0)
            load_x(0, 1)

            def batch(b, first, more):
                if not first:
                    store_y(b - 1, 1)
                if more:
                    sp.wait_ge(x1_ready, NJ * TT * (b + 1))
                    load_weighted(b + 1, 0, o_raw)
                    load_rinv(b + 1, 0, rinv)
                    sp.wait_ge(att_ready, NJ * (b + 1) + 1)
                    load_weighted(b + 1, 1, o_raw)
                    sp.wait_ge(att_lo_ready, NJ * (b + 1) + 1)
                    load_rinv(b + 1, 1, rinv)
                    load_x(b + 1, 0)
                    load_x(b + 1, 1)
                store_y(b, 0)

            batches(sp, batch)
            store_y(B - 1, 1)
            for j in range(NJ):
                sp.wait_ge(y_stored[j], 16 * B)

        @block.gpsimd
        def _(pool):
            with nc.allow_non_contiguous_dma(reason="a bias of one element per partition"):
                pool.dma_start(bv_sb[:], bv.rearrange("(t p) -> p t", p=P)).then_inc(bv_loaded, 16)
                for tile, array in ((b1, cn_b1), (b2, cn_b2), (b3, cn_b3), (gb1, gc_b1), (gb2, gc_b2)):
                    pool.dma_start(tile[:], array.rearrange("(t p) -> p t", p=P)).then_inc(small_loaded, 16)
                for tile, array in ((gate_x, g_xattn), (gate_f, g_ffn), (range_3, adaptive_range), (half_b4, cn_b4), (half_gb3, gc_b3),
                                    (gated_bo, bo)):
                    pool.dma_start(tile[:], array.partition_broadcast(P)).then_inc(small_loaded, 16)
                pool.dma_start(w4_col[:], cn_w4).then_inc(small_loaded, 16)
                pool.dma_start(gw3_col[:], gc_w3).then_inc(small_loaded, 16)
            make_identity(pool, ident, id_filled, id_ready)
            pool.memset(minus_half[:], -0.5).then_inc(id_filled, 1)
            pool.wait_ge(id_filled, 2)

            def normalise_attention(b, j):
                pool.wait_ge(o_loaded[j], 16 * (b + 1))
                pool.wait_ge(rinv_loaded[j], 16 * HPG * (b + 1))
                pool.tensor_tensor(rinv[:], o_raw[:], rinv[:], ALU.mult).then_inc(att_ready, 1)

            def add_bias(b, j):
                pool.wait_ge(x_loaded[j], 16 * (b + 1))
                pool.tensor_tensor(x_pre[j][:], x_pre[j][:], gated_bo[:].unsqueeze(1).to_broadcast([P, TT, E]),
                                   ALU.add).then_inc(xbo_ready, 1)

            def inverse_std(b, j):
                k = NJ * b + j
                held_wait(pool, mv_ready, k + 1, pool_passed)
                pool.tensor_scalar(var_eps[:], mv[:, :, 1], EPS, 1.0, ALU.add, ALU.mult).then_inc(var_ready, 1)
                pool.wait_ge(var_ready, k + 1)
                pool.tensor_tensor(rstd[:], var_eps[:], minus_half[:], ALU.pow).then_inc(rstd_ready, 1)

            pool.wait_ge(scaled, 4)
            add_bias(0, 0)
            add_bias(0, 1)

            def batch(b, first, more):
                inverse_std(b, 0)
                inverse_std(b, 1)
                if more:
                    normalise_attention(b + 1, 0)
                    normalise_attention(b + 1, 1)
                    add_bias(b + 1, 0)
                    add_bias(b + 1, 1)
                for j in range(NJ):
                    pool.wait_ge(coef_step, coef_steps(b, 1, j))
                    for m in range(ET):
                        pool.tensor_tensor(Bt[j][:, m, :], Bt[j][:, m, :], beta[:, j, :], ALU.mult).then_inc(B_scaled, 1)

            batches(pool, batch)

        @block.tensor
        def _(pe):
            def project(b, j, s):
                k = NJ * TT * b + TT * j + s
                if s == 0:
                    pe.wait_ge(att_lo_ready, NJ * b + j + 1)
                if j > 0:
                    pe.wait_ge(x1_ready, k - TT + 1)
                for t in range(ET):
                    last = three_pass(pe, acc[:, s, :], X_hi[j][:, t, s * P:(s + 1) * P], X_lo[j][:, t, s * P:(s + 1) * P],
                                      wo_hi[:, t, :], wo_lo[:, t, :], t == 0, t == ET - 1)
                last.then_inc(o_ready, 1)

            def transpose_x(b, j, tiles):
                if 0 in tiles:
                    pe.wait_ge(xn_ready, NJ * b + j + 1)
                for t in tiles:
                    wait(pe, xT_lo_ready, ET * (NJ * b + j) + t - 1)
                    for s in range(TT):
                        last = pe.transpose(tr[:, t % 2, s * P:(s + 1) * P], xn[j][:, s, t * P:(t + 1) * P], ident[:])
                    last.then_inc(xT_ready, 1)

            def first_layer(b, j, m):
                k = ET * (NJ * b + j) + m
                for twisted in range(2):
                    bank = (2 * m + twisted) % 4
                    if j == 0 and m < 2:
                        pe.wait_ge(x1_ready, NJ * TT * b + TT + bank + 1)
                    else:
                        pe.wait_ge((A_read, B_read)[twisted], k - 1)
                    cs = slice(m * P, (m + 1) * P)
                    for t in range(ET):
                        if m == 0 and not twisted:
                            pe.wait_ge(xT_lo_ready, ET * (NJ * b + j) + t + 1)
                        tile, sign = TWIST[t] if twisted else (t, 1)
                        w = (w1_hi[:, tile, cs], w1_lo[:, tile, cs]) if sign > 0 else (neg_hi[:, tile - 1, cs], neg_lo[:, tile - 1, cs])
                        last = three_pass(pe, acc[:, bank, :], w[0], w[1], X_hi[j][:, t, :], X_lo[j][:, t, :], t == 0, t == ET - 1)
                    last.then_inc((A_ready, B_ready)[twisted], 1)

            def global_layer1(b):
                pe.wait_ge(total_ready, b + 1)
                for m in range(2):
                    for t in range(ET):
                        last = pe.matmul(z4[:, 1, m:m + 1], gw1[:, t, m * P:(m + 1) * P], total[:, t:t + 1], start=t == 0, stop=t == ET - 1)
                last.then_inc(gz1_ready, 1)

            def global_layer2(b):
                pe.wait_ge(g1_ready, b + 1)
                for t in range(2):
                    last = pe.matmul(z4[:, 1, 2:3], gw2[:, t, :], g1[:, t:t + 1], start=t == 0, stop=t == 1)
                last.then_inc(gz2_ready, 1)

            def global_layer3(b):
                pe.wait_ge(g2_ready, b + 1)
                pe.matmul(z4[:, 1, 3:4], gw3[:], g2[:], start=True, stop=True).then_inc(gz3_ready, 1)

            def layer2(b, n, j, tiles):
                k = turn(b, n, j)
                if n == 0 and 0 in tiles:
                    pe.wait_ge(A_read, ET * NJ * (b + 1) - 1 + j)
                    pe.wait_ge(B_read, ET * NJ * (b + 1) - 1 + j)
                for t in tiles:
                    pe.wait_ge(h1_ready, ET * k + t + 1)
                    for m in range(2):
                        last = pe.matmul(acc[:, 2 * j + m, :], w2[:, t, m * P:(m + 1) * P], u[j][:, t, :], start=t == 0, stop=t == ET - 1)
                        if t == ET - 1:
                            last.then_inc(z2_ready, 1)

            def layer3(b, n, j):
                k = turn(b, n, j)
                for t in range(2):
                    pe.wait_ge(h2_ready, 2 * k + t + 1)
                    last = pe.matmul(tr[:, j, :], w3[:, t, :], h2[j][:, t, :], start=t == 0, stop=t == 1)
                last.then_inc(z3_ready, 1)

            def layer4(b, n, j):
                k = turn(b, n, j)
                pe.wait_ge(h3_ready, k + 1)
                if n == 0:
                    pe.wait_ge(g3_ready, b + 1)
                pe.matmul(z4[:, j, :], w4[:], h2[j][:, 0, :], start=True, stop=True).then_inc(z4_ready, 1)

            def columns(b, j):
                pe.wait_ge(coef_step, coef_steps(b, CYCLES - 1, j))
                for n, rowwise in enumerate((alpha, beta)):
                    for s in range(TT):
                        col = TT * n + s
                        last = pe.matmul(tr[:, j, col:col + 1], rowwise[:, j, s * P:(s + 1) * P], ident[:, 0:1], start=True, stop=True)
                last.then_inc(cols_ps_ready, 1)

            pe.wait_ge(id_ready, 1)
            pe.wait_ge(wo_hi_ready, 1)
            pe.wait_ge(wo_lo_ready, 1)

            def batch(b, first, more):
                project(b, 0, 0)
                project(b, 0, 1)
                if not first:
                    columns(b - 1, 1)
                project(b, 0, 2)
                project(b, 0, 3)
                project(b, 1, 0)
                project(b, 1, 1)
                project(b, 1, 2)
                transpose_x(b, 0, (0, 1))
                project(b, 1, 3)
                transpose_x(b, 0, (2, 3))
                if first:
                    pe.wait_ge(w1_lo_ready, 1)
                    pe.wait_ge(neg_ready, 2)
                first_layer(b, 0, 0)
                first_layer(b, 0, 1)
                transpose_x(b, 1, (0, 1))
                first_layer(b, 0, 2)
                transpose_x(b, 1, (2, 3))
                first_layer(b, 0, 3)
                first_layer(b, 1, 0)
                if first:
                    pe.wait_ge(w_loaded, 64)
                    pe.wait_ge(copied, 2)
                global_layer1(b)
                first_layer(b, 1, 1)
                first_layer(b, 1, 2)
                global_layer2(b)
                first_layer(b, 1, 3)
                global_layer3(b)
                layer2(b, 0, 0, (0,))
                for k in range(NJ * CYCLES):
                    n, j = k // NJ, k % NJ
                    layer2(b, n, j, (1, 2))
                    if k == NJ * CYCLES - 1:
                        columns(b, 0)
                    layer2(b, n, j, (3,))
                    layer3(b, n, j)
                    if k < NJ * CYCLES - 1:
                        layer2(b, (k + 1) // NJ, (k + 1) % NJ, (0,))
                    layer4(b, n, j)

            batches(pe, batch)
            columns(B - 1, 1)

        @block.scalar
        def _(act):
            act.dma_start(A[0][:], WoT.rearrange("(t p) f -> p t f", p=P)).then_inc(wo_loaded, 16)
            act.dma_start(A[1][:], cn_w1.rearrange("(t p) f -> p t f", p=P)).then_inc(w1_loaded, 16)

            def split_attention(b, j, source):
                act.wait_ge(att_ready, NJ * b + j + 1)
                wait(act, B_ready, ET * NJ * (b - 1) + ET * (j + 1))
                for t in range(ET):
                    last = act.activation(X_hi[j][:, t, :], source[:, t, :], ACT.Identity, bias=bv_sb[:, t:t + 1])
                last.then_inc(att_hi_ready, 1)

            act.wait_ge(wo_loaded, 16)
            act.activation(wo_hi[:], A[0][:], ACT.Copy).then_inc(wo_hi_ready, 1)
            act.wait_ge(bv_loaded, 16)
            split_attention(0, 0, rinv)
            act.wait_ge(small_loaded, 16 * 13)
            act.activation(gate_x[:], gate_x[:], ACT.Tanh).then_inc(gates_ready, 1)
            act.activation(gate_f[:], gate_f[:], ACT.Tanh).then_inc(gates_ready, 1)
            act.wait_ge(w1_loaded, 16)
            act.activation(w1_hi[:], A[1][:], ACT.Copy).then_inc(w1_hi_ready, 1)
            split_attention(0, 1, Bt[1])
            act.wait_ge(w1_hi_ready, 1)
            act.activation(neg_hi[:], w1_hi[:, 1:3, :].bitcast(F32), ACT.Copy, scale=-1.0).then_inc(neg_ready, 1)
            act.wait_ge(w1_lo_ready, 1)
            act.activation(neg_lo[:], w1_lo[:, 1:3, :].bitcast(F32), ACT.Copy, scale=-1.0).then_inc(neg_ready, 1)
            act.wait_ge(scaled, 4)

            def split_x(b, j, tiles):
                for t in tiles:
                    act.wait_ge(xT_ready, ET * (NJ * b + j) + t + 1)
                    act.activation(X_hi[j][:, t, :], tr[:, t % 2, :], ACT.Copy, accum_out=sums[:, j, t:t + 1]).then_inc(xT_hi_ready, 1)

            def first_cycle_h1(b, j, m):
                k = ET * (NJ * b + j) + m
                if m == 0:
                    wait(act, y_stored[j], 16 * b)
                act.wait_ge(A_ready, k + 1)
                act.activation(u[j][:, m, :], acc[:, (2 * m) % 4, :], ACT.Gelu, bias=b1[:, m:m + 1]).then_inc(h1_ready, 1)
                act.activation(A[j][:, m, :], acc[:, (2 * m) % 4, :], ACT.Copy).then_inc(A_read, 1)

            def h1(b, n, j, m):
                k = ((CYCLES - 1) * b + n - 1) * NJ + j
                act.wait_ge(u_ready, ET * k + m + 1)
                act.activation(u[j][:, m, :], u[j][:, m, :], ACT.Gelu, bias=b1[:, m:m + 1]).then_inc(h1_ready, 1)

            def h2_half(b, n, j, m):
                act.wait_ge(z2_ready, 2 * turn(b, n, j) + m + 1)
                act.activation(h2[j][:, m, :], acc[:, 2 * j + m, :], ACT.Gelu, bias=b2[:, m:m + 1]).then_inc(h2_ready, 1)

            def h3_all(b, n, j):
                act.wait_ge(z3_ready, turn(b, n, j) + 1)
                act.activation(h2[j][:, 0, :], tr[:, j, :], ACT.Gelu, bias=b3[:]).then_inc(h3_ready, 1)

            def gate(b, n, j):
                act.wait_ge(z4_ready, turn(b, n, j) + 1)
                act.activation(coef[:, j, :], z4[:, j, :], ACT.Tanh, scale=0.5, bias=half_b4[:]).then_inc(t_ready, 1)

            def batch(b, first, more):
                split_x(b, 0, range(ET))
                first_cycle_h1(b, 0, 0)
                first_cycle_h1(b, 0, 1)
                split_x(b, 1, (0, 1))
                first_cycle_h1(b, 0, 2)
                split_x(b, 1, (2, 3))
                first_cycle_h1(b, 0, 3)
                first_cycle_h1(b, 1, 0)
                act.wait_ge(gz1_ready, b + 1)
                for m in range(2):
                    last = act.activation(g1[:, m:m + 1], z4[:, 1, m:m + 1], ACT.Gelu, scale=1.0 / S, bias=gb1[:, m:m + 1])
                last.then_inc(g1_ready, 1)
                if more:
                    split_attention(b + 1, 0, rinv)
                first_cycle_h1(b, 1, 1)
                first_cycle_h1(b, 1, 2)
                act.wait_ge(gz2_ready, b + 1)
                act.activation(g2[:], z4[:, 1, 2:3], ACT.Gelu, bias=gb2[:]).then_inc(g2_ready, 1)
                first_cycle_h1(b, 1, 3)
                act.wait_ge(gz3_ready, b + 1)
                act.activation(g_tanh[:], z4[:, 1, 3:4], ACT.Tanh, scale=0.5, bias=half_gb3[:]).then_inc(g3_ready, 1)
                for k in range(NJ * CYCLES):
                    n, j = k // NJ, k % NJ
                    between = k > 0 and (k - 1) // NJ < CYCLES - 1
                    other = (b, (k - 1) // NJ + 1, (k - 1) % NJ)
                    h2_half(b, n, j, 0)
                    h2_half(b, n, j, 1)
                    if between:
                        h1(*other, 0)
                        h1(*other, 1)
                    if k == 0 and more:
                        split_attention(b + 1, 1, rinv)
                    h3_all(b, n, j)
                    if between:
                        h1(*other, 2)
                    gate(b, n, j)
                    if between:
                        h1(*other, 3)

            batches(act, batch)

        @block.vector
        def _(dve):
            def split_attention(b, j, source):
                dve.wait_ge(att_hi_ready, NJ * b + j + 1)
                for t in range(ET):
                    last = dve.scalar_tensor_tensor(X_lo[j][:, t, :], source[:, t, :], bv_sb[:, t:t + 1],
                                                    X_hi[j][:, t, :].bitcast(F32), ALU.add, ALU.subtract)
                last.then_inc(att_lo_ready, 1)

            dve.wait_ge(wo_hi_ready, 1)
            dve.tensor_tensor(wo_lo[:], A[0][:], wo_hi[:].bitcast(F32), ALU.subtract).then_inc(wo_lo_ready, 1)
            dve.wait_ge(o_loaded[0], 16)
            dve.wait_ge(rinv_loaded[0], 16 * HPG)
            dve.tensor_tensor(rinv[:], o_raw[:], rinv[:], ALU.mult).then_inc(att_ready, 1)
            split_attention(0, 0, rinv)
            dve.wait_ge(small_loaded, 16 * 13)
            dve.tensor_scalar(half_b4[:], half_b4[:], 0.5, None, ALU.mult).then_inc(scaled, 1)
            dve.tensor_scalar(half_gb3[:], half_gb3[:], 0.5, None, ALU.mult).then_inc(scaled, 1)
            dve.tensor_scalar(range_7[:], range_3[:], 0.7, None, ALU.mult).then_inc(scaled, 1)
            dve.wait_ge(gates_ready, 1)
            dve.tensor_scalar(gated_bo[:], gated_bo[:], gate_x[:], None, ALU.mult).then_inc(scaled, 1)
            dve.wait_ge(scaled, 3)
            dve.tensor_scalar(range_3[:], range_3[:], 0.3, None, ALU.mult).then_inc(copied, 1)
            dve.tensor_copy(w4[:], w4_col[:].to_broadcast([P, P])).then_inc(copied, 1)
            dve.tensor_copy(gw3[:], gw3_col[:].to_broadcast([P, P])).then_inc(copied, 1)
            dve.wait_ge(o_loaded[1], 16)
            dve.wait_ge(rinv_loaded[1], 16 * HPG)
            dve.tensor_tensor(Bt[1][:], Bt[0][:], Bt[1][:], ALU.mult).then_inc(att_ready, 1)
            split_attention(0, 1, Bt[1])
            dve.wait_ge(w1_hi_ready, 1)
            dve.tensor_tensor(w1_lo[:], A[1][:], w1_hi[:].bitcast(F32), ALU.subtract).then_inc(w1_lo_ready, 1)
            dve.wait_ge(copied, 3)

            def residual(b, j, s):
                k = NJ * TT * b + TT * j + s
                if s == 0:
                    dve.wait_ge(xbo_ready, NJ * b + j + 1)
                dve.wait_ge(o_ready, k + 1)
                dve.scalar_tensor_tensor(x1[j][:, s, :], acc[:, s, :], gate_x[:], x_pre[j][:, s, :], ALU.mult, ALU.add).then_inc(x1_ready, 1)
                dve.wait_ge(x1_ready, k + 1)
                last = dve.bn_stats(stats[:, s, :], x1[j][:, s, :])
                if s == TT - 1:
                    last.then_inc(stats_ready, 1)

            def mean_var(b, j):
                k = NJ * b + j
                held_wait(dve, stats_ready, k + 1, dve_passed)
                for s in range(TT):
                    last = dve.bn_aggr(mv[:, s, :], stats[:, s, :])
                last.then_inc(mv_ready, 1)

            def normalise(b, j):
                k = NJ * b + j
                dve.wait_ge(rstd_ready, k + 1)
                dve.wait_ge(mv_ready, k + 1)
                for s in range(TT):
                    last = dve.tensor_scalar(xn[j][:, s, :], x1[j][:, s, :], mv[:, s, 0:1], rstd[:, s:s + 1], ALU.subtract, ALU.mult)
                last.then_inc(xn_ready, 1)

            def split_x(b, j, tiles):
                for t in tiles:
                    dve.wait_ge(xT_hi_ready, ET * (NJ * b + j) + t + 1)
                    dve.tensor_tensor(X_lo[j][:, t, :], tr[:, t % 2, :], X_hi[j][:, t, :].bitcast(F32), ALU.subtract).then_inc(xT_lo_ready, 1)

            def read_B(b, j, m):
                dve.wait_ge(B_ready, ET * (NJ * b + j) + m + 1)
                dve.tensor_copy(Bt[j][:, m, :], acc[:, (2 * m + 1) % 4, :]).then_inc(B_read, 1)

            def coefficients(b, n, j):
                al, be, c = alpha[:, j, :], beta[:, j, :], coef[:, j, :]
                done = coef_steps(b, n, j) - (1, 4, 5)[n]
                dve.wait_ge(t_ready, turn(b, n, j) + 1)
                if n == 0:
                    if j == 0:
                        dve.wait_ge(base_ready, b + 1)
                    dve.tensor_scalar(be, c, range_3[:], base[:], ALU.mult, ALU.add).then_inc(coef_step, 1)
                    return
                dve.tensor_scalar(c, c, range_3[:], base[:], ALU.mult, ALU.add).then_inc(coef_step, 1)
                dve.wait_ge(coef_step, done + 1)
                dve.tensor_tensor(cross[:], c, be, ALU.mult).then_inc(coef_step, 1)
                if n == 1:
                    dve.tensor_tensor(be, be, c, ALU.add).then_inc(coef_step, 1)
                    dve.wait_ge(coef_step, done + 2)
                    dve.tensor_scalar(al, cross[:], -1.0, 1.0, ALU.mult, ALU.add).then_inc(coef_step, 1)
                else:
                    dve.tensor_tensor(c, c, al, ALU.mult).then_inc(coef_step, 1)
                    dve.wait_ge(coef_step, done + 2)
                    dve.tensor_tensor(al, al, cross[:], ALU.subtract).then_inc(coef_step, 1)
                    dve.wait_ge(coef_step, done + 3)
                    dve.tensor_tensor(be, be, c, ALU.add).then_inc(coef_step, 1)

            def mix(b, n, j):
                k = ET * (((CYCLES - 1) * b + n - 1) * NJ + j)
                dve.wait_ge(coef_step, coef_steps(b, n - 1, j))

                def multiply(m):
                    if n == 1:
                        dve.tensor_tensor(u[j][:, m, :], Bt[j][:, m, :], beta[:, j, :], ALU.mult).then_inc(mul_ready, 1)
                    else:
                        dve.tensor_tensor(u[j][:, m, :], A[j][:, m, :], alpha[:, j, :], ALU.mult).then_inc(mul_ready, 1)

                def add(m):
                    dve.wait_ge(mul_ready, k + m + 1)
                    if n == 2:
                        dve.wait_ge(B_scaled, ET * (NJ * b + j) + m + 1)
                    other = A if n == 1 else Bt
                    dve.tensor_tensor(u[j][:, m, :], u[j][:, m, :], other[j][:, m, :], ALU.add).then_inc(u_ready, 1)

                multiply(0)
                for m in range(1, ET):
                    multiply(m)
                    add(m - 1)
                add(ET - 1)

            def gated_columns(b, j):
                k = NJ * b + j
                dve.wait_ge(cols_ps_ready, k + 1)
                dve.tensor_scalar(cols[:, j, :], tr[:, j, 0:2 * TT], gate_f[:], None, ALU.mult).then_inc(cols_ready, 1)
                dve.wait_ge(cols_ready, 2 * k + 1)
                dve.tensor_scalar(neg_cols[:, j, :], cols[:, j, TT:2 * TT], -1.0, None, ALU.mult).then_inc(cols_ready, 1)
                dve.wait_ge(cols_ready, 2 * k + 2)

            def finish(b, j, s):
                k = TT * (NJ * b + j) + s
                dve.scalar_tensor_tensor(u[j][:, s, :], xn[j][:, s, :], cols[:, j, s:s + 1], x1[j][:, s, :], ALU.mult, ALU.add).then_inc(y_base, 1)
                dve.wait_ge(y_base, k + 1)
                for t in range(ET):
                    source, sign = ((2, 1), (3, -1), (0, -1), (1, 1))[t]
                    beta_s = cols[:, j, TT + s:TT + s + 1] if sign > 0 else neg_cols[:, j, s:s + 1]
                    last = dve.scalar_tensor_tensor(u[j][:, s, t * P:(t + 1) * P], xn[j][:, s, source * P:(source + 1) * P], beta_s,
                                                    u[j][:, s, t * P:(t + 1) * P], ALU.mult, ALU.add)
                if s == TT - 1:
                    last.then_inc(y_ready, 1)

            def batch(b, first, more):
                def finish_before(s):
                    if not first:
                        finish(b - 1, 1, s)

                residual(b, 0, 0)
                residual(b, 0, 1)
                if not first:
                    gated_columns(b - 1, 1)
                finish_before(0)
                residual(b, 0, 2)
                finish_before(1)
                residual(b, 0, 3)
                mean_var(b, 0)
                finish_before(2)
                normalise(b, 0)
                residual(b, 1, 0)
                residual(b, 1, 1)
                split_x(b, 0, (0, 1))
                finish_before(3)
                residual(b, 1, 2)
                split_x(b, 0, (2, 3))
                residual(b, 1, 3)
                mean_var(b, 1)
                normalise(b, 1)
                read_B(b, 0, 0)
                read_B(b, 0, 1)
                split_x(b, 1, (0, 1))
                read_B(b, 0, 2)
                split_x(b, 1, (2, 3))
                dve.wait_ge(xT_hi_ready, NJ * ET * (b + 1))
                dve.tensor_tensor(total[:], sums[:, 0, :], sums[:, 1, :], ALU.add).then_inc(total_ready, 1)
                read_B(b, 0, 3)
                read_B(b, 1, 0)
                read_B(b, 1, 1)
                if more:
                    split_attention(b + 1, 0, rinv)
                read_B(b, 1, 2)
                read_B(b, 1, 3)
                dve.wait_ge(g3_ready, b + 1)
                dve.tensor_scalar(base[:], g_tanh[:], range_7[:], BASE_COUPLING, ALU.mult, ALU.add).then_inc(base_ready, 1)
                for k in range(NJ * CYCLES):
                    n, j = k // NJ, k % NJ
                    coefficients(b, n, j)
                    if n < CYCLES - 1:
                        mix(b, n + 1, j)
                    elif j == 0:
                        gated_columns(b, 0)
                        for s in range(TT):
                            finish(b, 0, s)
                    if k == 0 and more:
                        split_attention(b + 1, 1, rinv)

            batches(dve, batch)
            gated_columns(B - 1, 1)
            for s in range(TT):
                finish(B - 1, 1, s)


INPUTS = ("x", "ctxT", "mask", "adj", "WqT", "bq", "WkT", "bk", "WvT", "g_xattn", "g_ffn", "bv", "WoT", "bo", "cn_w1", "cn_b1", "cn_w2",
          "cn_b2", "cn_w3", "cn_b3", "cn_w4", "cn_b4", "gc_w1", "gc_b1", "gc_w2", "gc_b2", "gc_w3", "gc_b3", "adaptive_range")


def gated_block(nc, x, ctxT, mask, adj, WqT, bq, WkT, bk, WvT, g_xattn, g_ffn, bv, WoT, bo, cn_w1, cn_b1, cn_w2, cn_b2, cn_w3, cn_b3,
                cn_w4, cn_b4, gc_w1, gc_b1, gc_w2, gc_b2, gc_w3, gc_b3, adaptive_range, out):
    def scratch(name, shape):
        return nc.dram_tensor(name, shape, F32, kind="Internal").ap()

    q_parts = scratch("q_parts", (2, E, TOK))
    k_parts = scratch("k_parts", (2, E, TOK))
    v_all = scratch("v_all", (TOK, E))
    o_all = scratch("o_all", (E, TOK))
    rinv_all = scratch("rinv_all", (B * H // HPG, HPG * S // P, P))
    project_phase(nc, x, ctxT, WqT, bq, WkT, bk, WvT, q_parts, k_parts, v_all)
    attention_phase(nc, adj, mask, q_parts, k_parts, v_all, o_all, rinv_all)
    ffn_phase(nc, x, o_all, rinv_all, g_xattn, g_ffn, bv, WoT, bo, cn_w1, cn_b1, cn_w2, cn_b2, cn_w3, cn_b3, cn_w4, cn_b4,
              gc_w1, gc_b1, gc_w2, gc_b2, gc_w3, gc_b3, adaptive_range, out)


def kernel(x, ctx_1024, mask_Bx1xSxS2_ik1, g_xattn, g_ffn, L0_xattn_adj, L0_xattn_Wq, L0_xattn_bq, L0_xattn_Wk, L0_xattn_bk,
           L0_xattn_Wv, L0_xattn_bv, L0_xattn_Wo, L0_xattn_bo, L0_ffn_adaptive_range, **ffn):
    import concourse.bacc as bacc
    from concourse.bass_utils import run_bass_kernel_spmd

    arrays = dict(
        x=x.reshape(TOK, E), mask=mask_Bx1xSxS2_ik1.reshape(TOK, S), adj=L0_xattn_adj,
        ctxT=ctx_1024.reshape(NCH, CH, E).transpose(0, 2, 1),
        WqT=L0_xattn_Wq.T, WkT=L0_xattn_Wk.T, WvT=L0_xattn_Wv.T, WoT=L0_xattn_Wo.T,
        bq=L0_xattn_bq, bk=L0_xattn_bk, bv=L0_xattn_bv, bo=L0_xattn_bo, g_xattn=g_xattn, g_ffn=g_ffn,
        adaptive_range=L0_ffn_adaptive_range)
    arrays.update({name[len("L0_ffn_"):]: array for name, array in ffn.items()})
    arrays = {name: np.ascontiguousarray(arrays[name]) for name in INPUTS}

    nc = bacc.Bacc("TRN2", target_bir_lowering=False, num_devices=1)
    args = {name: nc.dram_tensor(name, a.shape, mybir.dt.from_np(a.dtype), kind="ExternalInput").ap() for name, a in arrays.items()}
    out = nc.dram_tensor("out", (TOK, E), F32, kind="ExternalOutput").ap()
    gated_block(nc, out=out, **args)
    result = run_bass_kernel_spmd(nc, [arrays], core_ids=[0])
    return result.results[0]["out"].reshape(B, S, E)
```

```python
from contextlib import ExitStack

import numpy as np

import concourse.bass as bass
from concourse import mybir

P = 128
F32 = mybir.dt.float32
F32R = mybir.dt.float32r
I32 = mybir.dt.int32
ALU = mybir.AluOpType
ACT = mybir.ActivationFunctionType

B, S, E, H = 4, 1024, 512, 16
D = E // H
TOK = B * S
ET = E // P
HPG = P // D
CH = 512
NCH = TOK // CH
TT = CH // P
EPS = 1e-5
BASE_COUPLING = 0.1
INV_SQRT_D = float(np.float32(1.0) / np.sqrt(np.float32(D)))
QB = 256
Q_STACK = (0, 0, 1)
K_STACK = (0, 1, 0)
BIG = 3.0e38
ds = bass.ds


def wait(eng, sem, value):
    if isinstance(value, int) and value <= 0:
        return
    eng.wait_ge(sem, value)


def held_wait(eng, sem, value, passed):
    wait(eng, sem, value)
    if not isinstance(value, int):
        eng.sem_inc(passed, 1)


def make_identity(pool, ident, filled, ready):
    pool.memset(ident[:], 0.0).then_inc(filled, 1)
    pool.wait_ge(filled, 1)
    pool.affine_select(out=ident[:], in_=ident[:], compare_op=ALU.not_equal, fill=1.0,
                       base=0, pattern=[[-1, P]], channel_multiplier=1).then_inc(ready, 1)


def three_pass(pe, acc, w_hi, w_lo, r_hi, r_lo, first, last):
    pe.matmul(acc, w_hi, r_hi, start=first, stop=False)
    pe.matmul(acc, w_lo, r_hi, start=False, stop=False)
    return pe.matmul(acc, w_hi, r_lo, start=False, stop=last)


def project_phase(nc, x, ctxT, WqT, bq, WkT, bk, WvT, adj, mask, q_parts, k_parts, v_all, am, k_first, q_first, v_first):
    with ExitStack() as ctx:
        def sb(name, shape, dt=F32):
            return ctx.enter_context(nc.sbuf_tensor(name, shape, dt))

        def sem(name):
            return ctx.enter_context(nc.semaphore(name))

        stage = sb("p_stage", [P, 2, ET, E])
        w_hi = sb("p_w_hi", [P, 3, ET, E], F32R)
        w_lo = sb("p_w_lo", [P, 3, ET, E], F32R)
        x_raw = sb("p_x_raw", [P, TT, E])
        c_raw = sb("p_c_raw", [P, ET, CH])
        c_hi = sb("p_c_hi", [P, ET, CH], F32R)
        c_lo = sb("p_c_lo", [P, ET, CH], F32R)
        xn = sb("p_xn", [P, TT, E])
        xT_hi = sb("p_xT_hi", [P, ET, CH], F32R)
        xT_lo = sb("p_xT_lo", [P, ET, CH], F32R)
        out_hi = sb("p_out_hi", [P, ET, CH], F32R)
        out_lo = sb("p_out_lo", [P, ET, CH], F32R)
        v_out = sb("p_v_out", [P, TT, E])
        ident = sb("p_ident", [P, P])
        bias_q = sb("p_bias_q", [P, ET])
        bias_k = sb("p_bias_k", [P, ET])
        stats = sb("p_stats", [P, TT, 6])
        mv = sb("p_mv", [P, TT, 2])
        var_eps = sb("p_var_eps", [P, TT])
        rstd = sb("p_rstd", [P, TT])
        minus_half = sb("p_minus_half", [P, TT])
        acc = ctx.enter_context(nc.psum_tensor("p_acc", [P, 4, CH], F32))
        x_t = ctx.enter_context(nc.psum_tensor("p_x_t", [P, ET, CH], F32))

        w_loaded = [sem(f"p_w_loaded{n}") for n in range(3)]
        b_loaded = sem("p_b_loaded")
        x_loaded = sem("p_x_loaded")
        c_loaded = sem("p_c_loaded")
        c_tile_loaded = [sem(f"p_c_tile_loaded{t}") for t in range(ET)]
        wk_tile_loaded = [sem(f"p_wk_tile_loaded{t}") for t in range(ET)]
        id_filled = sem("p_id_filled")
        id_ready = sem("p_id_ready")
        bq_scaled = sem("p_bq_scaled")
        w_hi_ready = sem("p_w_hi_ready")
        w_lo_ready = sem("p_w_lo_ready")
        c_hi_ready = sem("p_c_hi_ready")
        c_lo_ready = sem("p_c_lo_ready")
        stats_ready = sem("p_stats_ready")
        mv_ready = sem("p_mv_ready")
        var_ready = sem("p_var_ready")
        rstd_ready = sem("p_rstd_ready")
        xn_ready = sem("p_xn_ready")
        xT_ready = sem("p_xT_ready")
        xT_hi_ready = sem("p_xT_hi_ready")
        xT_lo_ready = sem("p_xT_lo_ready")
        acc_ready = sem("p_acc_ready")
        acc_read = sem("p_acc_read")
        hi_ready = sem("p_hi_ready")
        q_done = sem("p_q_done")
        stored = [sem(f"p_stored{m}") for m in range(ET)]
        v_stored = sem("p_v_stored")
        first_loaded = sem("p_first_loaded")
        m_loaded = sem("p_m_loaded")
        adj_loaded = sem("p_adj_loaded")
        big_ready = sem("p_big_ready")
        am_built = sem("p_am_built")
        pool_passed = sem("p_pool_passed")
        dve_passed = sem("p_dve_passed")

        block = ctx.enter_context(nc.Block())
        NACC = 3 * 4
        w_raw = (stage[:, 0], stage[:, 1], v_out)
        mask_stage = stage[:, 0].rearrange("p (n t) f -> p n (t f)", n=2)[:, 0]
        adj_stage = stage[:, 1].rearrange("p (n t) f -> p n (t f)", n=2)[:, 0]

        @block.gpsimd
        def _(pool):
            pool.dma_start(x_raw[:], x[0:CH].rearrange("(t p) e -> p t e", p=P)).then_inc(x_loaded, 16)
            for n, array in ((1, WvT), (2, WqT)):
                pool.dma_start(w_raw[n][:], array.rearrange("(t p) f -> p t f", p=P)).then_inc(w_loaded[n], 16)
            make_identity(pool, ident, id_filled, id_ready)
            pool.memset(minus_half[:], -0.5).then_inc(id_filled, 1)
            pool.wait_ge(id_filled, 2)

            def inverse_std(c):
                held_wait(pool, mv_ready, c + 1, pool_passed)
                pool.tensor_scalar(var_eps[:], mv[:, :, 1], EPS, 1.0, ALU.add, ALU.mult).then_inc(var_ready, 1)
                pool.wait_ge(var_ready, c + 1)
                pool.tensor_tensor(rstd[:], var_eps[:], minus_half[:], ALU.pow).then_inc(rstd_ready, 1)

            def mask_tile(t):
                held_wait(pool, am_built, t, pool_passed)
                pool.dma_start(mask_stage.bitcast(I32), mask[ds(t * P, P), :]).then_inc(m_loaded, 16)
                pool.dma_start(adj_stage, adj[ds(t * P, P), :]).then_inc(adj_loaded, 16)
                held_wait(pool, m_loaded, 16 * (t + 1), pool_passed)
                pool.tensor_scalar(mask_stage, mask_stage.bitcast(I32), 0.0, -BIG, ALU.is_equal, ALU.mult).then_inc(big_ready, 1)
                pool.wait_ge(big_ready, t + 1)
                pool.wait_ge(adj_loaded, 16 * (t + 1))
                pool.tensor_tensor(am[:, ds(t, 1), :], mask_stage.unsqueeze(1), adj_stage.unsqueeze(1), ALU.add).then_inc(am_built, 1)

            inverse_std(0)
            pool.wait_ge(w_lo_ready, 2 * ET)
            mask_tile(0)
            with pool.Fori(1, NCH) as c:
                pool.wait_ge(xn_ready, c)
                pool.dma_start(x_raw[:], x[ds(c * CH, CH), :].rearrange("(t p) e -> p t e", p=P)).then_inc(x_loaded, 16)
                pool.wait_ge(c_lo_ready, ET * c)
                pool.dma_start(c_raw[:], ctxT[ds(c, 1)].rearrange("a (t p) s -> p (a t) s", p=P)).then_inc(c_loaded, 16)
                inverse_std(c)
                mask_tile(c)
            pool.wait_ge(stored[0], 64 * S // CH)
            pool.wait_ge(v_stored, 16 * S // CH)
            for quad, part in enumerate(K_STACK):
                pool.dma_start(k_first[quad * D:(quad + 1) * D], k_parts[part, 0:P, 0:S].rearrange("(h d) s -> d h s", d=D)).then_inc(first_loaded, 16)
            for quad, part in enumerate(Q_STACK):
                pool.dma_start(q_first[quad * D:(quad + 1) * D], q_parts[part, 0:P, 0:QB].rearrange("(h d) s -> d h s", d=D)).then_inc(first_loaded, 16)
            pool.dma_start(v_first[:], v_all[0:S, 0:P].rearrange("(t p) f -> p t f", p=P)).then_inc(first_loaded, 16)
            pool.wait_ge(first_loaded, 16 * 7)

        @block.sync
        def _(sp):
            for t in range(ET):
                sp.dma_start(c_raw[:, t, :], ctxT[0, t * P:(t + 1) * P, :]).then_inc(c_tile_loaded[t], 16)
            with nc.allow_non_contiguous_dma(reason="a bias of one element per partition"):
                sp.dma_start(bias_q[:], bq.rearrange("(t p) -> p t", p=P)).then_inc(b_loaded, 16)
                sp.dma_start(bias_k[:], bk.rearrange("(t p) -> p t", p=P)).then_inc(b_loaded, 16)

            def store_parts(c, parts, n0, h0):
                for m in range(ET):
                    def tile(part):
                        return parts[part, m * P:(m + 1) * P, ds(c * CH, CH)]

                    sp.wait_ge(hi_ready, 2 * ET * c + h0 + m + 1)
                    sp.dma_start(tile(0), out_hi[:, m, :].bitcast(F32)).then_inc(stored[m], 16)
                    sp.wait_ge(acc_read, NACC * c + n0 + m + 1 + 4)
                    sp.dma_start(tile(1), out_lo[:, m, :].bitcast(F32)).then_inc(stored[m], 16)

            with sp.Fori(0, NCH) as c:
                store_parts(c, k_parts, 0, 0)
                sp.wait_ge(acc_read, NACC * c + 8 + 4)
                sp.dma_start(v_all[ds(c * CH, CH), :].rearrange("(t p) f -> p t f", p=P), v_out[:]).then_inc(v_stored, 16)
                store_parts(c, q_parts, 8, ET)
            for m in range(ET):
                sp.wait_ge(stored[m], 64 * NCH)
            sp.wait_ge(v_stored, 16 * NCH)

        @block.tensor
        def _(pe):
            def product(c, n, lhs, rhs):
                pe.wait_ge(acc_read, NACC * c + n + 1)
                for t in range(ET):
                    if n == 0:
                        pe.wait_ge(c_lo_ready, ET * c + t + 1)
                        if isinstance(c, int):
                            pe.wait_ge(w_lo_ready, t + 1)
                    last = three_pass(pe, acc[:, n % 4, :], lhs(0, t), lhs(1, t), rhs(0, t), rhs(1, t), t == 0, t == ET - 1)
                return last

            def chunk(c, first):
                cs = (c_hi, c_lo)
                xs = (xT_hi, xT_lo)
                for m in range(4):
                    w = lambda part, t: (w_hi, w_lo)[part][:, 0, t, m * P:(m + 1) * P]
                    product(c, m, w, lambda part, t: cs[part][:, t, :]).then_inc(acc_ready, 1)
                if first:
                    pe.wait_ge(id_ready, 1)
                pe.wait_ge(xn_ready, c + 1)
                for t in range(ET):
                    for s in range(TT):
                        last = pe.transpose(x_t[:, t, s * P:(s + 1) * P], xn[:, s, t * P:(t + 1) * P], ident[:])
                    last.then_inc(xT_ready, 1)
                if first:
                    pe.wait_ge(w_lo_ready, 2 * ET)
                for m in range(4):
                    w = lambda part, t: cs[part][:, t, m * P:(m + 1) * P]
                    product(c, 4 + m, w, lambda part, t: (w_hi, w_lo)[part][:, 1, t, :]).then_inc(acc_ready, 1)
                if first:
                    pe.wait_ge(w_lo_ready, 3 * ET)
                pe.wait_ge(xT_hi_ready, 4 * c + 4)
                pe.wait_ge(xT_lo_ready, 4 * c + 4)
                for m in range(4):
                    w = lambda part, t: (w_hi, w_lo)[part][:, 2, t, m * P:(m + 1) * P]
                    product(c, 8 + m, w, lambda part, t: xs[part][:, t, :]).then_inc(acc_ready, 1)

            chunk(0, True)
            with pe.Fori(1, NCH) as c:
                chunk(c, False)

        @block.scalar
        def _(act):
            for t in range(ET):
                act.dma_start(w_raw[0][:, t, :], WkT[t * P:(t + 1) * P, :]).then_inc(wk_tile_loaded[t], 16)
            for t in range(ET):
                act.wait_ge(c_tile_loaded[t], 16)
                act.activation(c_hi[:, t, :], c_raw[:, t, :], ACT.Copy).then_inc(c_hi_ready, 1)
                act.wait_ge(wk_tile_loaded[t], 16)
                act.activation(w_hi[:, 0, t, :], w_raw[0][:, t, :], ACT.Copy).then_inc(w_hi_ready, 1)

            def split_context(c):
                act.wait_ge(c_loaded, 16 * c)
                wait(act, acc_ready, NACC * c - 4)
                act.activation(c_hi[:], c_raw[:], ACT.Copy).then_inc(c_hi_ready, ET)

            def split_weight(n):
                act.wait_ge(w_loaded[n], 16)
                act.activation(w_hi[:, n], w_raw[n][:], ACT.Copy, scale=INV_SQRT_D if n == 2 else 1.0).then_inc(w_hi_ready, ET)

            split_weight(1)
            split_weight(2)
            act.wait_ge(b_loaded, 32)
            act.wait_ge(bq_scaled, 1)

            def high_parts(c, n0, bias):
                for m in range(4):
                    wait(act, stored[m], 64 * c + (32 if n0 else 0))
                    act.wait_ge(acc_ready, NACC * c + n0 + m + 1)
                    act.activation(out_hi[:, m, :], acc[:, (n0 + m) % 4, :], ACT.Identity,
                                   bias=bias[:, m:m + 1]).then_inc(hi_ready, 1)

            def chunk(c, more):
                high_parts(c, 0, bias_k)
                for t in range(ET):
                    act.wait_ge(xT_ready, 4 * c + t + 1)
                    act.activation(xT_hi[:, t, :], x_t[:, t, :], ACT.Copy).then_inc(xT_hi_ready, 1)
                if more:
                    split_context(c + 1)
                high_parts(c, 8, bias_q)

            chunk(0, True)
            with act.Fori(1, NCH - 1) as c:
                chunk(c, True)
            chunk(NCH - 1, False)

        @block.vector
        def _(dve):
            dve.sem_inc(acc_read, 4)

            def norm_stats(c):
                dve.wait_ge(x_loaded, 16 * (c + 1))
                for s in range(TT):
                    last = dve.bn_stats(stats[:, s, :], x_raw[:, s, :])
                last.then_inc(stats_ready, 1)
                held_wait(dve, stats_ready, c + 1, dve_passed)
                for s in range(TT):
                    last = dve.bn_aggr(mv[:, s, :], stats[:, s, :])
                last.then_inc(mv_ready, 1)

            def norm_apply(c):
                dve.wait_ge(rstd_ready, c + 1)
                wait(dve, xT_ready, 4 * c)
                dve.wait_ge(mv_ready, c + 1)
                for s in range(TT):
                    last = dve.tensor_scalar(xn[:, s, :], x_raw[:, s, :], mv[:, s, 0:1], rstd[:, s:s + 1], ALU.subtract, ALU.mult)
                last.then_inc(xn_ready, 1)

            def split_context(c):
                dve.wait_ge(c_hi_ready, ET * (c + 1))
                dve.tensor_tensor(c_lo[:], c_raw[:], c_hi[:].bitcast(F32), ALU.subtract).then_inc(c_lo_ready, ET)

            def split_weight(n):
                dve.wait_ge(w_hi_ready, ET * (n + 1))
                dve.scalar_tensor_tensor(w_lo[:, n], w_raw[n][:], INV_SQRT_D if n == 2 else 1.0, w_hi[:, n].bitcast(F32),
                                         ALU.mult, ALU.subtract).then_inc(w_lo_ready, ET)

            for t in range(ET):
                dve.wait_ge(c_hi_ready, t + 1)
                dve.tensor_tensor(c_lo[:, t, :], c_raw[:, t, :], c_hi[:, t, :].bitcast(F32), ALU.subtract).then_inc(c_lo_ready, 1)
                dve.wait_ge(w_hi_ready, t + 1)
                dve.tensor_tensor(w_lo[:, 0, t, :], w_raw[0][:, t, :], w_hi[:, 0, t, :].bitcast(F32), ALU.subtract).then_inc(w_lo_ready, 1)
            dve.wait_ge(b_loaded, 32)
            dve.tensor_scalar(bias_q[:], bias_q[:], INV_SQRT_D, None, ALU.mult).then_inc(bq_scaled, 1)
            dve.wait_ge(bq_scaled, 1)
            norm_stats(0)
            split_weight(1)
            norm_apply(0)
            split_weight(2)

            def low_parts(c, n0, h0, bias):
                for m in range(4):
                    wait(dve, stored[m], 64 * c + (32 if n0 else 0))
                    dve.wait_ge(hi_ready, 8 * c + h0 + m + 1)
                    dve.scalar_tensor_tensor(out_lo[:, m, :], acc[:, (n0 + m) % 4, :], bias[:, m:m + 1],
                                             out_hi[:, m, :].bitcast(F32), ALU.add, ALU.subtract).then_inc(acc_read, 1)

            def chunk(c, more):
                low_parts(c, 0, 0, bias_k)
                for t in range(ET):
                    dve.wait_ge(xT_hi_ready, 4 * c + t + 1)
                    dve.tensor_tensor(xT_lo[:, t, :], x_t[:, t, :], xT_hi[:, t, :].bitcast(F32), ALU.subtract).then_inc(xT_lo_ready, 1)
                wait(dve, v_stored, 16 * c)
                for m in range(4):
                    dve.wait_ge(acc_ready, NACC * c + 4 + m + 1)
                    dve.tensor_copy(v_out[:, m, :], acc[:, m, :]).then_inc(acc_read, 1)
                if more:
                    norm_stats(c + 1)
                    split_context(c + 1)
                    norm_apply(c + 1)
                low_parts(c, 8, 4, bias_q)

            chunk(0, True)
            with dve.Fori(1, NCH - 1) as c:
                chunk(c, True)
            chunk(NCH - 1, False)


def attention_phase(nc, adj, mask, q_parts, k_parts, v_all, am, k_first, q_first, v_first, o_all, rinv_all):
    NQB = S // QB
    UB = HPG * QB // P
    UG = UB * NQB
    NG = B * H // HPG
    NU = NG * UG
    PAIR = 2 * UG
    NPAIR = NU // PAIR
    LEAD = 2 * UB
    GPB = H // HPG
    BPB = GPB * NQB
    KT = S // P
    NPROB = 4
    AHEAD = 3
    ACT_LAG, DVE_LAG = 1, 2
    STACK = 3 * D

    with ExitStack() as ctx:
        def sb(name, shape, dt=F32):
            return ctx.enter_context(nc.sbuf_tensor(name, shape, dt))

        def sem(name):
            return ctx.enter_context(nc.semaphore(name))

        q_st = [q_first] + [sb(f"a_q_st{n}", [P, HPG, QB], F32R) for n in range(1, NQB)]
        k_st = [k_first, sb("a_k_st1", [P, HPG, S], F32R)]
        v_sb = [v_first, sb("a_v1", [P, KT, P])]
        neg = sb("a_neg", [P, 2, S])
        prob = sb("a_prob", [P, NPROB, S])
        probT = sb("a_probT", [P, 2, HPG, KT, QB])
        o_sb = sb("a_o", [P, 2, QB])
        m_raw = sb("a_m_raw", [P, 2, S], I32)
        adj_raw = sb("a_adj_raw", [P, 2, S])
        row_min = sb("a_row_min", [P, 2])
        row_sum = sb("a_row_sum", [P, 2, UG])
        rinv = sb("a_rinv", [P, P])
        rinvT = sb("a_rinvT", [UG, P])
        ident = sb("a_ident", [P, P])
        sc_ps = ctx.enter_context(nc.psum_tensor("a_sc_ps", [P, 2, S], F32))
        tr_ps = ctx.enter_context(nc.psum_tensor("a_tr_ps", [P, 2, 4 * P], F32))
        o_ps = ctx.enter_context(nc.psum_tensor("a_o_ps", [P, 2, 512], F32))

        q_loaded = [sem(f"a_q_loaded{n}") for n in range(NQB)]
        k_loaded = [sem(f"a_k_loaded{n}") for n in range(2)]
        v_loaded = [sem(f"a_v_loaded{n}") for n in range(2)]
        adj_loaded = [sem(f"a_adj_loaded{n}") for n in range(2)]
        m_loaded = [sem(f"a_m_loaded{n}") for n in range(2)]
        id_filled = sem("a_id_filled")
        id_ready = sem("a_id_ready")
        rinv_filled = sem("a_rinv_filled")
        big_ready = sem("a_big_ready")
        am_ready = sem("a_am_ready")
        am_built = sem("a_am_built")
        sc_ready = sem("a_sc_ready")
        neg_ready = sem("a_neg_ready")
        prob_ready = sem("a_prob_ready")
        tr_ready = [sem(f"a_tr_ready{n}") for n in range(2)]
        tr_read = [sem(f"a_tr_read{n}") for n in range(2)]
        pv_ready = sem("a_pv_ready")
        o_ready = sem("a_o_ready")
        rinv_ready = sem("a_rinv_ready")
        rinvT_ps_ready = sem("a_rinvT_ps_ready")
        rinvT_ready = sem("a_rinvT_ready")
        o_stored = [sem(f"a_o_stored{n}") for n in range(2)]
        rinv_stored = sem("a_rinv_stored")
        pool_passed = sem("a_pool_passed")
        dve_passed = sem("a_dve_passed")
        sp_passed = sem("a_sp_passed")

        block = ctx.enter_context(nc.Block())

        def run(eng, step):
            for r in range(LEAD):
                step(0, r)
            with eng.Fori(0, NPAIR - 1) as i:
                for v in range(LEAD, LEAD + PAIR):
                    step(i + v // PAIR, v % PAIR)
            for r in range(LEAD, PAIR):
                step(NPAIR - 1, r)

        def shifted(p, r, k):
            return p + (r + k) // PAIR, (r + k) % PAIR

        def exists(p, r):
            return not (isinstance(p, int) and (PAIR * p + r < 0 or PAIR * p + r >= NU))

        def parts(p, r):
            return PAIR * p + r, (PAIR // UB) * p + r // UB, 2 * p + r // UG

        @block.sync
        def _(sp):
            for n in range(2):
                sp.sem_inc(o_stored[n], 16)
            sp.sem_inc(rinv_stored, 16)

            def load_v(b, g):
                G = GPB * b + g
                held_wait(sp, pv_ready, NQB * (G - 1), sp_passed)
                sp.dma_start(v_sb[g % 2][:], v_all[ds(b * S, S), g * P:(g + 1) * P].rearrange("(t p) f -> p t f", p=P)
                             ).then_inc(v_loaded[g % 2], 16)

            def store_o(b, g, qb, first):
                k = NQB * g + qb - 2
                if first and k < 0:
                    return
                bb, k = (b, k) if k >= 0 else (b - 1, k + BPB)
                gg, qq = k // NQB, k % NQB
                n = BPB * bb + k
                held_wait(sp, o_ready, n + 2, sp_passed)
                sp.dma_start(o_all[gg * P:(gg + 1) * P, ds(bb * S + qq * QB, QB)], o_sb[:, k % 2]).then_inc(o_stored[k % 2], 16)

            def store_rinv(G):
                sp.wait_ge(rinvT_ready, G + 1)
                sp.dma_start(rinv_all[ds(G, 1)].rearrange("a r s -> (a r) s"), rinvT[:]).then_inc(rinv_stored, 16)

            def load_masks(b, t):
                n = KT * (b - 1) + t
                if not (isinstance(n, int) and n < 2):
                    held_wait(sp, am_built, n - 1, sp_passed)
                sp.dma_start(m_raw[:, t % 2, :], mask[ds(b * S + t * P, P), :]).then_inc(m_loaded[t % 2], 16)
                sp.dma_start(adj_raw[:, t % 2, :], adj[t * P:(t + 1) * P, :]).then_inc(adj_loaded[t % 2], 16)

            def batch(b, first):
                for g in range(GPB):
                    if not (first and g == 0):
                        load_v(b, g)
                    for qb in range(NQB):
                        if not (first and g == 0):
                            gg, bb = (g - 1, b) if g else (GPB - 1, b - 1)
                            store_o(bb, gg, qb, first and g == 1)
                            if qb == NQB - 1 and not (first and g == 1):
                                store_rinv(GPB * bb + gg - 1)
                        if not first and g == 0:
                            load_masks(b, 2 * qb)
                            load_masks(b, 2 * qb + 1)

            batch(0, True)
            batch(1, False)
            with sp.Fori(2, B) as b:
                batch(b, False)
            for qb in range(NQB):
                store_o(B - 1, GPB - 1, qb, False)
            store_rinv(NG - 2)
            store_o(B, 0, 0, False)
            store_o(B, 0, 1, False)
            store_rinv(NG - 1)
            for n in range(2):
                sp.wait_ge(o_stored[n], 16 * NG * NQB // 2 + 16)
            sp.wait_ge(rinv_stored, 16 * (NG + 1))

        @block.gpsimd
        def _(pool):
            make_identity(pool, ident, id_filled, id_ready)
            pool.sem_inc(am_ready, BPB)

            def load_k(b, g):
                G = GPB * b + g
                held_wait(pool, sc_ready, UG * (G - 1), pool_passed)
                for quad, part in enumerate(K_STACK):
                    src = k_parts[part, g * P:(g + 1) * P, ds(b * S, S)].rearrange("(h d) s -> d h s", d=D)
                    pool.dma_start(k_st[g % 2][quad * D:(quad + 1) * D], src).then_inc(k_loaded[g % 2], 16)

            def load_q(b, g, qb):
                G = GPB * b + g
                held_wait(pool, sc_ready, UG * (G - 1) + UB * (qb + 1), pool_passed)
                for quad, part in enumerate(Q_STACK):
                    src = q_parts[part, g * P:(g + 1) * P, ds(b * S + qb * QB, QB)].rearrange("(h d) s -> d h s", d=D)
                    pool.dma_start(q_st[qb][quad * D:(quad + 1) * D], src).then_inc(q_loaded[qb], 16)

            def minus_infinity(b, t):
                held_wait(pool, m_loaded[t % 2], 16 * (KT // 2 * (b - 1) + t // 2 + 1), pool_passed)
                pool.tensor_scalar(m_raw[:, t % 2, :].bitcast(F32), m_raw[:, t % 2, :], 0.0, -BIG,
                                   ALU.is_equal, ALU.mult).then_inc(big_ready, 1)

            def add_adj(b, t):
                n = KT * (b - 1) + t
                pool.wait_ge(big_ready, n + 1)
                pool.wait_ge(adj_loaded[t % 2], 16 * (KT // 2 * (b - 1) + t // 2 + 1))
                pool.wait_ge(neg_ready, (GPB * b - 1) * UG + UB * (t // 2 + 1))
                pool.tensor_tensor(am[:, t, :], m_raw[:, t % 2, :].bitcast(F32), adj_raw[:, t % 2, :], ALU.add).then_inc(am_built, 1)

            def batch(b, first):
                for g in range(GPB):
                    if g:
                        load_k(b, g)
                    for qb in range(NQB):
                        masks = g == 0 and not first
                        if masks:
                            minus_infinity(b, 2 * qb)
                            minus_infinity(b, 2 * qb + 1)
                            if qb == 0:
                                load_k(b, g)
                        if not (first and g == 0 and qb == 0):
                            load_q(b, g, qb)
                        if masks:
                            add_adj(b, 2 * qb)
                            add_adj(b, 2 * qb + 1)
                            pool.wait_ge(am_built, KT * (b - 1) + 2 * qb + 2)
                            pool.sem_inc(am_ready, 1)
                    if g == 0 and not first:
                        pool.sem_inc(am_ready, BPB - NQB)

            batch(0, True)
            with pool.Fori(1, B) as b:
                batch(b, False)

        @block.tensor
        def _(pe):
            pe.sem_inc(rinvT_ps_ready, 1)
            pe.wait_ge(id_ready, 1)

            def scores(p, r):
                if not exists(p, r):
                    return
                u, blk, G = parts(p, r)
                par, qb, h, qt = r // UG, (r // UB) % NQB, r % UB // 2, r % 2
                if r % UG == 0:
                    wait(pe, k_loaded[par], 48 * (p + par))
                if r % UB == 0:
                    wait(pe, q_loaded[qb], 48 * (2 * p + par + (qb > 0)))
                wait(pe, neg_ready, u - 1)
                for half in range(2):
                    last = pe.matmul(sc_ps[:, r % 2, half * 512:(half + 1) * 512],
                                     q_st[qb][0:STACK, h, qt * P:(qt + 1) * P],
                                     k_st[par][0:STACK, h, half * 512:(half + 1) * 512], start=True, stop=True)
                last.then_inc(sc_ready, 1)

            def transposes(p, r, half):
                u, _, _ = parts(p, r)
                if half == 0:
                    pe.wait_ge(prob_ready, u + 1)
                wait(pe, tr_read[half], u)
                for j in range(4):
                    t = 4 * half + j
                    last = pe.transpose(tr_ps[:, half, j * P:(j + 1) * P], prob[:, r % NPROB, t * P:(t + 1) * P], ident[:])
                last.then_inc(tr_ready[half], 1)

            def weighted_values(p, r):
                u, blk, _ = parts(p, r)
                t = r % UB
                prev = r // UB - 1
                if isinstance(p, int) and p == 0 and prev < 0:
                    return
                vpar = (prev // NQB) % 2 if prev >= 0 else 1
                if t % 4 == 0:
                    pe.wait_ge(tr_read[t // 4], UB * blk)
                if t == 0:
                    wait(pe, o_ready, blk - 1)
                    if prev % NQB == 0:
                        wait(pe, v_loaded[vpar], 16 * (p + vpar))
                    if r == UB or r == UB + UG:
                        wait(pe, rinvT_ready, 2 * p + r // UG)
                for h in range(HPG):
                    last = pe.matmul(o_ps[h * D:(h + 1) * D, prev % 2, 0:QB], v_sb[vpar][:, t, h * D:(h + 1) * D],
                                     probT[:, prev % 2, h, t, :], start=(t == 0), stop=(t == KT - 1))
                if t == KT - 1:
                    last.then_inc(pv_ready, 1)

            def transpose_rinv(G, first):
                if first:
                    return
                pe.wait_ge(rinv_ready, G)
                pe.wait_ge(o_ready, NQB * G)
                pe.transpose(o_ps[:, 0, QB:QB + P], rinv[:], ident[:]).then_inc(rinvT_ps_ready, 1)

            def step(p, r):
                transposes(p, r, 0)
                transposes(p, r, 1)
                scores(*shifted(p, r, AHEAD))
                weighted_values(p, r)
                if r % UG == 3:
                    transpose_rinv(2 * p + r // UG, isinstance(p, int) and p == 0 and r < UG)

            for r in range(AHEAD):
                scores(0, r)
            run(pe, step)
            for r in range(UB):
                weighted_values(NPAIR, r)
            transpose_rinv(NG, False)

        @block.scalar
        def _(act):
            def read_transposes(p, r):
                if not exists(p, r):
                    return
                u, _, _ = parts(p, r)
                h, qt = r % UB // 2, r % 2
                act.wait_ge(tr_ready[0], u + 1)
                if r % UB == 0:
                    wait(act, pv_ready, (PAIR // UB) * p + r // UB - 1)
                act.activation(probT[:, (r // UB) % 2, h, 0:4, qt * P:(qt + 1) * P],
                               tr_ps[:, 0, :].rearrange("p (t q) -> p t q", t=4), ACT.Copy).then_inc(tr_read[0], 1)

            act.sem_inc(o_ready, 1)

            def read_output(blk, par, first):
                if first:
                    return
                act.wait_ge(pv_ready, blk + 1)
                act.wait_ge(o_stored[par], 8 * (blk - par) + 16)
                act.activation(o_sb[:, par, :], o_ps[:, par, 0:QB], ACT.Copy).then_inc(o_ready, 1)

            def step(p, r):
                u, blk, _ = parts(p, r)
                qb, h, qt = (r // UB) % NQB, r % UB // 2, r % 2
                col = h * KT + 2 * qb + qt
                act.wait_ge(neg_ready, u + 1)
                for half in range(2):
                    wait(act, tr_ready[half], u - NPROB + 1)
                act.activation(prob[:, r % NPROB, :], neg[:, r % 2, :], ACT.Exp, scale=-1.0, bias=row_min[:, r % 2:r % 2 + 1],
                               accum_out=row_sum[:, r // UG, col:col + 1]).then_inc(prob_ready, 1)
                read_transposes(*shifted(p, r, -ACT_LAG))
                if r % UB == 1:
                    read_output(blk - 2, (r // UB) % 2, isinstance(p, int) and p == 0 and r // UB < 2)

            run(act, step)
            for k in range(ACT_LAG, 0, -1):
                read_transposes(NPAIR - 1, PAIR - k)
            read_output(NU // UB - 2, 0, False)
            read_output(NU // UB - 1, 1, False)

        @block.vector
        def _(dve):
            dve.memset(rinv[:], 1.0).then_inc(rinv_filled, 1)
            dve.wait_ge(rinv_filled, 1)

            def read_transposes(p, r):
                if not exists(p, r):
                    return
                u, _, _ = parts(p, r)
                h, qt = r % UB // 2, r % 2
                if r % UB == 0:
                    wait(dve, pv_ready, (PAIR // UB) * p + r // UB - 1)
                dve.wait_ge(tr_ready[1], u + 1)
                dve.tensor_copy(probT[:, (r // UB) % 2, h, 4:8, qt * P:(qt + 1) * P],
                                tr_ps[:, 1, :].rearrange("p (t q) -> p t q", t=4)).then_inc(tr_read[1], 1)

            def inverse_sums(G, par, first):
                if first:
                    return
                dve.wait_ge(prob_ready, UG * G)
                wait(dve, rinvT_ps_ready, G)
                dve.reciprocal(rinv[:, 0:UG], row_sum[:, par, :]).then_inc(rinv_ready, 1)

            def read_rinv(G, first):
                if first:
                    return
                dve.wait_ge(rinvT_ps_ready, G + 1)
                dve.wait_ge(rinv_stored, 16 * G)
                dve.tensor_copy(rinvT[:], o_ps[0:UG, 0, QB:QB + P]).then_inc(rinvT_ready, 1)

            def step(p, r):
                u, blk, G = parts(p, r)
                qb, qt = (r // UB) % NQB, r % 2
                first = isinstance(p, int) and p == 0
                if r % UB == 0:
                    dve.wait_ge(am_ready, blk + 1)
                wait(dve, prob_ready, u - 1)
                held_wait(dve, sc_ready, u + 1, dve_passed)
                dve.tensor_tensor_reduce(out=neg[:, r % 2, :], in0=sc_ps[:, r % 2, :], in1=am[:, 2 * qb + qt, :],
                                         scale=-1.0, scalar=3.4e38, op0=ALU.add, op1=ALU.min,
                                         accum_out=row_min[:, r % 2:r % 2 + 1]).then_inc(neg_ready, 1)
                read_transposes(*shifted(p, r, -DVE_LAG))
                if r % UG == 3:
                    inverse_sums(G, 1 - r // UG, first and r < UG)
                if r % UG == 7:
                    read_rinv(G, first and r < UG)

            run(dve, step)
            for k in range(DVE_LAG, 0, -1):
                read_transposes(NPAIR - 1, PAIR - k)
            inverse_sums(NG, 1, False)
            read_rinv(NG, False)


def ffn_phase(nc, x, o_all, rinv_all, g_xattn, g_ffn, bv, WoT, bo, cn_w1, cn_b1, cn_w2, cn_b2, cn_w3, cn_b3, cn_w4, cn_b4,
              gc_w1, gc_b1, gc_w2, gc_b2, gc_w3, gc_b3, adaptive_range, out):
    NJ = S // CH
    F2, F3 = E // 2, E // 4
    CYCLES = 3
    GPB = H // HPG
    TWIST = ((2, -1), (3, 1), (0, 1), (1, -1))

    with ExitStack() as ctx:
        def sb(name, shape, dt=F32):
            return ctx.enter_context(nc.sbuf_tensor(name, shape, dt))

        def ps(name, shape):
            return ctx.enter_context(nc.psum_tensor(name, shape, F32))

        def sem(name):
            return ctx.enter_context(nc.semaphore(name))

        wo_hi = sb("f_wo_hi", [P, ET, E], F32R)
        wo_lo = sb("f_wo_lo", [P, ET, E], F32R)
        w1_hi = sb("f_w1_hi", [P, ET, E], F32R)
        w1_lo = sb("f_w1_lo", [P, ET, E], F32R)
        neg_hi = sb("f_neg_hi", [P, 2, E], F32R)
        neg_lo = sb("f_neg_lo", [P, 2, E], F32R)
        w2 = sb("f_w2", [P, ET, F2])
        w3 = sb("f_w3", [P, 2, F3])
        w4_col = sb("f_w4_col", [P, 1])
        w4 = sb("f_w4", [P, P])
        gw1 = sb("f_gw1", [P, ET, F2])
        gw2 = sb("f_gw2", [P, 2, F3])
        gw3_col = sb("f_gw3_col", [P, 1])
        gw3 = sb("f_gw3", [P, P])
        b1 = sb("f_b1", [P, ET])
        b2 = sb("f_b2", [P, 2])
        b3 = sb("f_b3", [P, 1])
        half_b4 = sb("f_half_b4", [P, 1])
        gb1 = sb("f_gb1", [P, 2])
        gb2 = sb("f_gb2", [P, 1])
        half_gb3 = sb("f_half_gb3", [P, 1])
        bv_sb = sb("f_bv", [P, ET])
        gate_x = sb("f_gate_x", [P, 1])
        gate_f = sb("f_gate_f", [P, 1])
        range_3 = sb("f_range_3", [P, 1])
        range_7 = sb("f_range_7", [P, 1])
        gated_bo = sb("f_gated_bo", [P, E])
        ident = sb("f_ident", [P, P])

        X_hi = [sb(f"f_X_hi{j}", [P, ET, CH], F32R) for j in range(NJ)]
        X_lo = [sb(f"f_X_lo{j}", [P, ET, CH], F32R) for j in range(NJ)]
        o_raw = sb("f_o_raw", [P, ET, CH])
        rinv = sb("f_rinv", [P, ET, CH])

        def at_start(b):
            return isinstance(b, int) and b == 0

        def x_before(b):
            return xn if at_start(b) else (o_raw, rinv)

        x1 = [sb(f"f_x1_{j}", [P, TT, E]) for j in range(NJ)]
        xn = [sb(f"f_xn{j}", [P, TT, E]) for j in range(NJ)]
        A = [sb(f"f_A{j}", [P, ET, CH]) for j in range(NJ)]
        Bt = [sb(f"f_B{j}", [P, ET, CH]) for j in range(NJ)]
        u = [sb(f"f_u{j}", [P, ET, CH]) for j in range(NJ)]
        h2 = [sb(f"f_h2_{j}", [P, 2, CH]) for j in range(NJ)]
        coef = sb("f_coef", [P, NJ, CH])
        alpha = sb("f_alpha", [P, NJ, CH])
        beta = sb("f_beta", [P, NJ, CH])
        cross = sb("f_cross", [P, CH])
        stats = sb("f_stats", [P, TT, 6])
        mv = sb("f_mv", [P, TT, 2])
        var_eps = sb("f_var_eps", [P, TT])
        rstd = sb("f_rstd", [P, TT])
        minus_half = sb("f_minus_half", [P, TT])
        sums = sb("f_sums", [P, NJ, ET])
        total = sb("f_total", [P, ET])
        g1 = sb("f_g1", [P, 2])
        g2 = sb("f_g2", [P, 1])
        g_tanh = sb("f_g_tanh", [P, 1])
        base = sb("f_base", [P, 1])
        cols = sb("f_cols", [P, NJ, 2 * TT])
        neg_cols = sb("f_neg_cols", [P, NJ, TT])

        acc = ps("f_acc", [P, 4, CH])
        tr = ps("f_tr", [P, 2, CH])
        z4 = ps("f_z4", [P, NJ, CH])

        small_loaded = sem("f_small_loaded")
        early_loaded = sem("f_early_loaded")
        gate_x_ready = sem("f_gate_x_ready")
        bo_ready = sem("f_bo_ready")
        wo_loaded = sem("f_wo_loaded")
        w1_loaded = sem("f_w1_loaded")
        w_loaded = sem("f_w_loaded")
        o_loaded = [sem(f"f_o_loaded{j}") for j in range(NJ)]
        rinv_loaded = [sem(f"f_rinv_loaded{j}") for j in range(NJ)]
        x_loaded = [sem(f"f_x_loaded{j}") for j in range(NJ)]
        y_stored = [sem(f"f_y_stored{j}") for j in range(NJ)]
        id_filled = sem("f_id_filled")
        id_ready = sem("f_id_ready")
        gate_f_ready = sem("f_gate_f_ready")
        scaled = sem("f_scaled")
        copied = sem("f_copied")
        wo_hi_ready = sem("f_wo_hi_ready")
        wo_lo_ready = sem("f_wo_lo_ready")
        w1_hi_ready = sem("f_w1_hi_ready")
        w1_lo_ready = sem("f_w1_lo_ready")
        neg_ready = sem("f_neg_ready")
        att_ready = sem("f_att_ready")
        att_hi_ready = sem("f_att_hi_ready")
        att_lo_ready = sem("f_att_lo_ready")
        o_ready = sem("f_o_ready")
        xbo_ready = sem("f_xbo_ready")
        x1_ready = sem("f_x1_ready")
        stats_ready = sem("f_stats_ready")
        mv_ready = sem("f_mv_ready")
        var_ready = sem("f_var_ready")
        rstd_ready = sem("f_rstd_ready")
        xn_ready = sem("f_xn_ready")
        xT_ready = sem("f_xT_ready")
        xT_hi_ready = sem("f_xT_hi_ready")
        xT_lo_ready = sem("f_xT_lo_ready")
        A_ready = sem("f_A_ready")
        B_ready = sem("f_B_ready")
        A_read = sem("f_A_read")
        B_read = sem("f_B_read")
        total_ready = sem("f_total_ready")
        gz1_ready = sem("f_gz1_ready")
        g1_ready = sem("f_g1_ready")
        gz2_ready = sem("f_gz2_ready")
        g2_ready = sem("f_g2_ready")
        gz3_ready = sem("f_gz3_ready")
        g3_ready = sem("f_g3_ready")
        base_ready = sem("f_base_ready")
        mul_ready = sem("f_mul_ready")
        B_scaled = sem("f_B_scaled")
        u_ready = sem("f_u_ready")
        h1_ready = sem("f_h1_ready")
        z2_ready = sem("f_z2_ready")
        h2_ready = sem("f_h2_ready")
        z3_ready = sem("f_z3_ready")
        h3_ready = sem("f_h3_ready")
        z4_ready = sem("f_z4_ready")
        t_ready = sem("f_t_ready")
        coef_step = sem("f_coef_step")
        cols_ps_ready = sem("f_cols_ps_ready")
        cols_ready = sem("f_cols_ready")
        y_base = sem("f_y_base")
        y_ready = sem("f_y_ready")
        pool_passed = sem("f_pool_passed")
        dve_passed = sem("f_dve_passed")
        block = ctx.enter_context(nc.Block())

        def turn(b, n, j):
            return (CYCLES * b + n) * NJ + j

        def coef_steps(b, n, j):
            per_cycle = (1, 4, 5)
            return NJ * sum(per_cycle) * b + NJ * sum(per_cycle[:n]) + per_cycle[n] * (j + 1)

        def batches(eng, body):
            body(0, True, True)
            with eng.Fori(1, B - 1) as b:
                body(b, False, True)
            body(B - 1, False, False)

        def rows(array, b, j):
            return array[ds(b * S + j * CH, CH), :].rearrange("(t p) e -> p t e", p=P)

        @block.sync
        def _(sp):
            def load_weighted(b, j, tile):
                sp.dma_start(tile[:], o_all.rearrange("(t p) s -> p t s", p=P)[:, :, ds(b * S + j * CH, CH)]).then_inc(o_loaded[j], 16)

            def load_rinv(b, j, tile):
                for h in range(HPG):
                    row = h * (S // P) + j * TT
                    sp.dma_start(tile[h * D:(h + 1) * D], rinv_all[ds(b * GPB, GPB), row:row + TT, :].rearrange(
                        "t q s -> t (q s)").partition_broadcast(D)).then_inc(rinv_loaded[j], 16)

            def load_x(b, j):
                if not at_start(b):
                    sp.wait_ge(att_ready if j == 0 else att_lo_ready, ET * NJ * (b + 1))
                sp.dma_start(x_before(b)[j][:], rows(x, b, j)).then_inc(x_loaded[j], 16)

            def store_y(b, j):
                sp.wait_ge(y_ready, NJ * b + j + 1)
                sp.dma_start(rows(out, b, j), u[j][:]).then_inc(y_stored[j], 16)

            load_weighted(0, 0, o_raw)
            load_rinv(0, 0, rinv)
            load_x(0, 0)
            load_weighted(0, 1, Bt[0])
            load_rinv(0, 1, Bt[1])
            load_x(0, 1)
            sp.dma_start(A[1][:], cn_w1.rearrange("(t p) f -> p t f", p=P)).then_inc(w1_loaded, 16)
            for tile, array in ((w2, cn_w2), (w3, cn_w3), (gw1, gc_w1), (gw2, gc_w2)):
                sp.dma_start(tile[:], array.rearrange("(t p) f -> p t f", p=P)).then_inc(w_loaded, 16)

            def batch(b, first, more):
                if not first:
                    store_y(b - 1, 1)
                if more:
                    sp.wait_ge(x1_ready, NJ * TT * (b + 1))
                    load_weighted(b + 1, 0, o_raw)
                    load_rinv(b + 1, 0, rinv)
                    sp.wait_ge(att_ready, ET * (NJ * (b + 1) + 1))
                    load_weighted(b + 1, 1, o_raw)
                    sp.wait_ge(att_lo_ready, ET * (NJ * (b + 1) + 1))
                    load_rinv(b + 1, 1, rinv)
                    load_x(b + 1, 0)
                    load_x(b + 1, 1)
                store_y(b, 0)

            batches(sp, batch)
            store_y(B - 1, 1)
            for j in range(NJ):
                sp.wait_ge(y_stored[j], 16 * B)

        @block.gpsimd
        def _(pool):
            with nc.allow_non_contiguous_dma(reason="a bias of one element per partition"):
                pool.dma_start(bv_sb[:], bv.rearrange("(t p) -> p t", p=P)).then_inc(early_loaded, 16)
                pool.dma_start(gate_x[:], g_xattn.partition_broadcast(P)).then_inc(early_loaded, 16)
                pool.dma_start(gated_bo[:], bo.partition_broadcast(P)).then_inc(early_loaded, 16)
                for tile, array in ((b1, cn_b1), (b2, cn_b2), (b3, cn_b3), (gb1, gc_b1), (gb2, gc_b2)):
                    pool.dma_start(tile[:], array.rearrange("(t p) -> p t", p=P)).then_inc(small_loaded, 16)
                for tile, array in ((gate_f, g_ffn), (range_3, adaptive_range), (half_b4, cn_b4), (half_gb3, gc_b3)):
                    pool.dma_start(tile[:], array.partition_broadcast(P)).then_inc(small_loaded, 16)
                pool.dma_start(w4_col[:], cn_w4).then_inc(small_loaded, 16)
                pool.dma_start(gw3_col[:], gc_w3).then_inc(small_loaded, 16)
            make_identity(pool, ident, id_filled, id_ready)
            pool.memset(minus_half[:], -0.5).then_inc(id_filled, 1)
            pool.wait_ge(id_filled, 2)

            def normalise_attention(b, j):
                pool.wait_ge(o_loaded[j], 16 * (b + 1))
                pool.wait_ge(rinv_loaded[j], 16 * HPG * (b + 1))
                pool.tensor_tensor(rinv[:], o_raw[:], rinv[:], ALU.mult).then_inc(att_ready, ET)

            def add_bias(b, j):
                pool.wait_ge(x_loaded[j], 16 * (b + 1))
                pool.tensor_tensor(x_before(b)[j][:], x_before(b)[j][:], gated_bo[:].unsqueeze(1).to_broadcast([P, TT, E]),
                                   ALU.add).then_inc(xbo_ready, 1)

            def inverse_std(b, j):
                k = NJ * b + j
                held_wait(pool, mv_ready, k + 1, pool_passed)
                pool.tensor_scalar(var_eps[:], mv[:, :, 1], EPS, 1.0, ALU.add, ALU.mult).then_inc(var_ready, 1)
                pool.wait_ge(var_ready, k + 1)
                pool.tensor_tensor(rstd[:], var_eps[:], minus_half[:], ALU.pow).then_inc(rstd_ready, 1)

            pool.wait_ge(bo_ready, 1)
            add_bias(0, 0)
            add_bias(0, 1)

            def batch(b, first, more):
                inverse_std(b, 0)
                inverse_std(b, 1)
                if more:
                    normalise_attention(b + 1, 0)
                    normalise_attention(b + 1, 1)
                    add_bias(b + 1, 0)
                    add_bias(b + 1, 1)
                for j in range(NJ):
                    pool.wait_ge(coef_step, coef_steps(b, 1, j))
                    for m in range(ET):
                        pool.tensor_tensor(Bt[j][:, m, :], Bt[j][:, m, :], beta[:, j, :], ALU.mult).then_inc(B_scaled, 1)

            batches(pool, batch)

        @block.tensor
        def _(pe):
            def project(b, j, s):
                k = NJ * TT * b + TT * j + s
                if j > 0:
                    pe.wait_ge(x1_ready, k - TT + 1)
                for t in range(ET):
                    if s == 0:
                        pe.wait_ge(att_lo_ready, ET * (NJ * b + j) + t + 1)
                    last = three_pass(pe, acc[:, s, :], X_hi[j][:, t, s * P:(s + 1) * P], X_lo[j][:, t, s * P:(s + 1) * P],
                                      wo_hi[:, t, :], wo_lo[:, t, :], t == 0, t == ET - 1)
                last.then_inc(o_ready, 1)

            def transpose_x(b, j, tiles):
                if 0 in tiles:
                    pe.wait_ge(xn_ready, NJ * b + j + 1)
                for t in tiles:
                    wait(pe, xT_lo_ready, ET * (NJ * b + j) + t - 1)
                    for s in range(TT):
                        last = pe.transpose(tr[:, t % 2, s * P:(s + 1) * P], xn[j][:, s, t * P:(t + 1) * P], ident[:])
                    last.then_inc(xT_ready, 1)

            def first_layer(b, j, m):
                k = ET * (NJ * b + j) + m
                for twisted in range(2):
                    bank = (2 * m + twisted) % 4
                    if j == 0 and m < 2:
                        pe.wait_ge(x1_ready, NJ * TT * b + TT + bank + 1)
                    else:
                        pe.wait_ge((A_read, B_read)[twisted], k - 1)
                    cs = slice(m * P, (m + 1) * P)
                    for t in range(ET):
                        if m == 0 and not twisted:
                            pe.wait_ge(xT_lo_ready, ET * (NJ * b + j) + t + 1)
                        tile, sign = TWIST[t] if twisted else (t, 1)
                        w = (w1_hi[:, tile, cs], w1_lo[:, tile, cs]) if sign > 0 else (neg_hi[:, tile - 1, cs], neg_lo[:, tile - 1, cs])
                        last = three_pass(pe, acc[:, bank, :], w[0], w[1], X_hi[j][:, t, :], X_lo[j][:, t, :], t == 0, t == ET - 1)
                    last.then_inc((A_ready, B_ready)[twisted], 1)

            def global_layer1(b):
                pe.wait_ge(total_ready, b + 1)
                for m in range(2):
                    for t in range(ET):
                        last = pe.matmul(z4[:, 1, m:m + 1], gw1[:, t, m * P:(m + 1) * P], total[:, t:t + 1], start=t == 0, stop=t == ET - 1)
                last.then_inc(gz1_ready, 1)

            def global_layer2(b):
                pe.wait_ge(g1_ready, b + 1)
                for t in range(2):
                    last = pe.matmul(z4[:, 1, 2:3], gw2[:, t, :], g1[:, t:t + 1], start=t == 0, stop=t == 1)
                last.then_inc(gz2_ready, 1)

            def global_layer3(b):
                pe.wait_ge(g2_ready, b + 1)
                pe.matmul(z4[:, 1, 3:4], gw3[:], g2[:], start=True, stop=True).then_inc(gz3_ready, 1)

            def layer2(b, n, j, tiles):
                k = turn(b, n, j)
                if n == 0 and 0 in tiles:
                    pe.wait_ge(A_read, ET * NJ * (b + 1) - 1 + j)
                    pe.wait_ge(B_read, ET * NJ * (b + 1) - 1 + j)
                for t in tiles:
                    pe.wait_ge(h1_ready, ET * k + t + 1)
                    for m in range(2):
                        last = pe.matmul(acc[:, 2 * j + m, :], w2[:, t, m * P:(m + 1) * P], u[j][:, t, :], start=t == 0, stop=t == ET - 1)
                        if t == ET - 1:
                            last.then_inc(z2_ready, 1)

            def layer3(b, n, j):
                k = turn(b, n, j)
                for t in range(2):
                    pe.wait_ge(h2_ready, 2 * k + t + 1)
                    last = pe.matmul(tr[:, j, :], w3[:, t, :], h2[j][:, t, :], start=t == 0, stop=t == 1)
                last.then_inc(z3_ready, 1)

            def layer4(b, n, j):
                k = turn(b, n, j)
                pe.wait_ge(h3_ready, k + 1)
                if n == 0:
                    pe.wait_ge(g3_ready, b + 1)
                pe.matmul(z4[:, j, :], w4[:], h2[j][:, 0, :], start=True, stop=True).then_inc(z4_ready, 1)

            def columns(b, j):
                pe.wait_ge(coef_step, coef_steps(b, CYCLES - 1, j))
                for n, rowwise in enumerate((alpha, beta)):
                    for s in range(TT):
                        col = TT * n + s
                        last = pe.matmul(tr[:, j, col:col + 1], rowwise[:, j, s * P:(s + 1) * P], ident[:, 0:1], start=True, stop=True)
                last.then_inc(cols_ps_ready, 1)

            pe.wait_ge(id_ready, 1)
            pe.wait_ge(wo_hi_ready, 1)
            pe.wait_ge(wo_lo_ready, 1)

            def batch(b, first, more):
                project(b, 0, 0)
                project(b, 0, 1)
                if not first:
                    columns(b - 1, 1)
                project(b, 0, 2)
                project(b, 0, 3)
                project(b, 1, 0)
                project(b, 1, 1)
                project(b, 1, 2)
                transpose_x(b, 0, (0, 1))
                project(b, 1, 3)
                transpose_x(b, 0, (2, 3))
                if first:
                    pe.wait_ge(w1_lo_ready, 1)
                    pe.wait_ge(neg_ready, 2)
                first_layer(b, 0, 0)
                first_layer(b, 0, 1)
                transpose_x(b, 1, (0, 1))
                first_layer(b, 0, 2)
                transpose_x(b, 1, (2, 3))
                first_layer(b, 0, 3)
                first_layer(b, 1, 0)
                if first:
                    pe.wait_ge(w_loaded, 64)
                    pe.wait_ge(copied, 2)
                global_layer1(b)
                first_layer(b, 1, 1)
                first_layer(b, 1, 2)
                global_layer2(b)
                first_layer(b, 1, 3)
                global_layer3(b)
                layer2(b, 0, 0, (0,))
                for k in range(NJ * CYCLES):
                    n, j = k // NJ, k % NJ
                    layer2(b, n, j, (1, 2))
                    if k == NJ * CYCLES - 1:
                        columns(b, 0)
                    layer2(b, n, j, (3,))
                    layer3(b, n, j)
                    if k < NJ * CYCLES - 1:
                        layer2(b, (k + 1) // NJ, (k + 1) % NJ, (0,))
                    layer4(b, n, j)

            batches(pe, batch)
            columns(B - 1, 1)

        @block.scalar
        def _(act):
            act.dma_start(A[0][:], WoT.rearrange("(t p) f -> p t f", p=P)).then_inc(wo_loaded, 16)

            def split_attention(b, j, source):
                wait(act, B_ready, ET * NJ * (b - 1) + ET * (j + 1))
                for t in range(ET):
                    act.wait_ge(att_ready, ET * (NJ * b + j) + t + 1)
                    act.activation(X_hi[j][:, t, :], source[:, t, :], ACT.Identity, bias=bv_sb[:, t:t + 1]).then_inc(att_hi_ready, 1)

            act.wait_ge(wo_loaded, 16)
            act.activation(wo_hi[:], A[0][:], ACT.Copy).then_inc(wo_hi_ready, 1)
            act.wait_ge(early_loaded, 48)
            act.activation(gate_x[:], gate_x[:], ACT.Tanh).then_inc(gate_x_ready, 1)
            split_attention(0, 0, rinv)
            split_attention(0, 1, Bt[1])
            act.wait_ge(small_loaded, 16 * 11)
            act.activation(gate_f[:], gate_f[:], ACT.Tanh).then_inc(gate_f_ready, 1)
            act.wait_ge(w1_loaded, 16)
            act.activation(w1_hi[:], A[1][:], ACT.Copy).then_inc(w1_hi_ready, 1)
            act.wait_ge(w1_hi_ready, 1)
            act.activation(neg_hi[:], w1_hi[:, 1:3, :].bitcast(F32), ACT.Copy, scale=-1.0).then_inc(neg_ready, 1)
            act.wait_ge(w1_lo_ready, 1)
            act.activation(neg_lo[:], w1_lo[:, 1:3, :].bitcast(F32), ACT.Copy, scale=-1.0).then_inc(neg_ready, 1)
            act.wait_ge(scaled, 3)

            def split_x(b, j, tiles):
                for t in tiles:
                    act.wait_ge(xT_ready, ET * (NJ * b + j) + t + 1)
                    act.activation(X_hi[j][:, t, :], tr[:, t % 2, :], ACT.Copy, accum_out=sums[:, j, t:t + 1]).then_inc(xT_hi_ready, 1)

            def first_cycle_h1(b, j, m):
                k = ET * (NJ * b + j) + m
                if m == 0:
                    wait(act, y_stored[j], 16 * b)
                act.wait_ge(A_ready, k + 1)
                act.activation(u[j][:, m, :], acc[:, (2 * m) % 4, :], ACT.Gelu, bias=b1[:, m:m + 1]).then_inc(h1_ready, 1)
                act.activation(A[j][:, m, :], acc[:, (2 * m) % 4, :], ACT.Copy).then_inc(A_read, 1)

            def h1(b, n, j, m):
                k = ((CYCLES - 1) * b + n - 1) * NJ + j
                act.wait_ge(u_ready, ET * k + m + 1)
                act.activation(u[j][:, m, :], u[j][:, m, :], ACT.Gelu, bias=b1[:, m:m + 1]).then_inc(h1_ready, 1)

            def h2_half(b, n, j, m):
                act.wait_ge(z2_ready, 2 * turn(b, n, j) + m + 1)
                act.activation(h2[j][:, m, :], acc[:, 2 * j + m, :], ACT.Gelu, bias=b2[:, m:m + 1]).then_inc(h2_ready, 1)

            def h3_all(b, n, j):
                act.wait_ge(z3_ready, turn(b, n, j) + 1)
                act.activation(h2[j][:, 0, :], tr[:, j, :], ACT.Gelu, bias=b3[:]).then_inc(h3_ready, 1)

            def gate(b, n, j):
                act.wait_ge(z4_ready, turn(b, n, j) + 1)
                act.activation(coef[:, j, :], z4[:, j, :], ACT.Tanh, scale=0.5, bias=half_b4[:]).then_inc(t_ready, 1)

            def batch(b, first, more):
                split_x(b, 0, range(ET))
                first_cycle_h1(b, 0, 0)
                first_cycle_h1(b, 0, 1)
                split_x(b, 1, (0, 1))
                first_cycle_h1(b, 0, 2)
                split_x(b, 1, (2, 3))
                first_cycle_h1(b, 0, 3)
                first_cycle_h1(b, 1, 0)
                act.wait_ge(gz1_ready, b + 1)
                for m in range(2):
                    last = act.activation(g1[:, m:m + 1], z4[:, 1, m:m + 1], ACT.Gelu, scale=1.0 / S, bias=gb1[:, m:m + 1])
                last.then_inc(g1_ready, 1)
                if more:
                    split_attention(b + 1, 0, rinv)
                first_cycle_h1(b, 1, 1)
                first_cycle_h1(b, 1, 2)
                act.wait_ge(gz2_ready, b + 1)
                act.activation(g2[:], z4[:, 1, 2:3], ACT.Gelu, bias=gb2[:]).then_inc(g2_ready, 1)
                first_cycle_h1(b, 1, 3)
                act.wait_ge(gz3_ready, b + 1)
                act.activation(g_tanh[:], z4[:, 1, 3:4], ACT.Tanh, scale=0.5, bias=half_gb3[:]).then_inc(g3_ready, 1)
                for k in range(NJ * CYCLES):
                    n, j = k // NJ, k % NJ
                    between = k > 0 and (k - 1) // NJ < CYCLES - 1
                    other = (b, (k - 1) // NJ + 1, (k - 1) % NJ)
                    h2_half(b, n, j, 0)
                    h2_half(b, n, j, 1)
                    if between:
                        h1(*other, 0)
                        h1(*other, 1)
                    if k == 0 and more:
                        split_attention(b + 1, 1, rinv)
                    h3_all(b, n, j)
                    if between:
                        h1(*other, 2)
                    gate(b, n, j)
                    if between:
                        h1(*other, 3)

            batches(act, batch)

        @block.vector
        def _(dve):
            def split_attention(b, j, source):
                for t in range(ET):
                    dve.wait_ge(att_hi_ready, ET * (NJ * b + j) + t + 1)
                    dve.scalar_tensor_tensor(X_lo[j][:, t, :], source[:, t, :], bv_sb[:, t:t + 1],
                                             X_hi[j][:, t, :].bitcast(F32), ALU.add, ALU.subtract).then_inc(att_lo_ready, 1)

            dve.wait_ge(wo_hi_ready, 1)
            dve.tensor_tensor(wo_lo[:], A[0][:], wo_hi[:].bitcast(F32), ALU.subtract).then_inc(wo_lo_ready, 1)
            dve.wait_ge(o_loaded[0], 16)
            dve.wait_ge(rinv_loaded[0], 16 * HPG)
            for t in range(ET):
                dve.tensor_tensor(rinv[:, t, :], o_raw[:, t, :], rinv[:, t, :], ALU.mult).then_inc(att_ready, 1)
            split_attention(0, 0, rinv)
            dve.wait_ge(gate_x_ready, 1)
            dve.tensor_scalar(gated_bo[:], gated_bo[:], gate_x[:], None, ALU.mult).then_inc(bo_ready, 1)
            dve.wait_ge(o_loaded[1], 16)
            dve.wait_ge(rinv_loaded[1], 16 * HPG)
            dve.tensor_tensor(Bt[1][:], Bt[0][:], Bt[1][:], ALU.mult).then_inc(att_ready, ET)
            split_attention(0, 1, Bt[1])
            def prepare_weights():
                dve.wait_ge(small_loaded, 16 * 11)
                dve.tensor_scalar(half_b4[:], half_b4[:], 0.5, None, ALU.mult).then_inc(scaled, 1)
                dve.tensor_scalar(half_gb3[:], half_gb3[:], 0.5, None, ALU.mult).then_inc(scaled, 1)
                dve.tensor_scalar(range_7[:], range_3[:], 0.7, None, ALU.mult).then_inc(scaled, 1)
                dve.wait_ge(scaled, 3)
                dve.tensor_scalar(range_3[:], range_3[:], 0.3, None, ALU.mult).then_inc(copied, 1)
                dve.tensor_copy(w4[:], w4_col[:].to_broadcast([P, P])).then_inc(copied, 1)
                dve.tensor_copy(gw3[:], gw3_col[:].to_broadcast([P, P])).then_inc(copied, 1)
                dve.wait_ge(w1_hi_ready, 1)
                dve.tensor_tensor(w1_lo[:], A[1][:], w1_hi[:].bitcast(F32), ALU.subtract).then_inc(w1_lo_ready, 1)
                dve.wait_ge(copied, 3)
                dve.wait_ge(gate_f_ready, 1)

            def residual(b, j, s):
                k = NJ * TT * b + TT * j + s
                if s == 0:
                    dve.wait_ge(xbo_ready, NJ * b + j + 1)
                dve.wait_ge(o_ready, k + 1)
                dve.scalar_tensor_tensor(x1[j][:, s, :], acc[:, s, :], gate_x[:], x_before(b)[j][:, s, :], ALU.mult, ALU.add).then_inc(x1_ready, 1)
                dve.wait_ge(x1_ready, k + 1)
                last = dve.bn_stats(stats[:, s, :], x1[j][:, s, :])
                if s == TT - 1:
                    last.then_inc(stats_ready, 1)

            def mean_var(b, j):
                k = NJ * b + j
                held_wait(dve, stats_ready, k + 1, dve_passed)
                for s in range(TT):
                    last = dve.bn_aggr(mv[:, s, :], stats[:, s, :])
                last.then_inc(mv_ready, 1)

            def normalise(b, j):
                k = NJ * b + j
                dve.wait_ge(rstd_ready, k + 1)
                dve.wait_ge(mv_ready, k + 1)
                for s in range(TT):
                    last = dve.tensor_scalar(xn[j][:, s, :], x1[j][:, s, :], mv[:, s, 0:1], rstd[:, s:s + 1], ALU.subtract, ALU.mult)
                last.then_inc(xn_ready, 1)

            def split_x(b, j, tiles):
                for t in tiles:
                    dve.wait_ge(xT_hi_ready, ET * (NJ * b + j) + t + 1)
                    dve.tensor_tensor(X_lo[j][:, t, :], tr[:, t % 2, :], X_hi[j][:, t, :].bitcast(F32), ALU.subtract).then_inc(xT_lo_ready, 1)

            def read_B(b, j, m):
                dve.wait_ge(B_ready, ET * (NJ * b + j) + m + 1)
                dve.tensor_copy(Bt[j][:, m, :], acc[:, (2 * m + 1) % 4, :]).then_inc(B_read, 1)

            def coefficients(b, n, j):
                al, be, c = alpha[:, j, :], beta[:, j, :], coef[:, j, :]
                done = coef_steps(b, n, j) - (1, 4, 5)[n]
                dve.wait_ge(t_ready, turn(b, n, j) + 1)
                if n == 0:
                    if j == 0:
                        dve.wait_ge(base_ready, b + 1)
                    dve.tensor_scalar(be, c, range_3[:], base[:], ALU.mult, ALU.add).then_inc(coef_step, 1)
                    return
                dve.tensor_scalar(c, c, range_3[:], base[:], ALU.mult, ALU.add).then_inc(coef_step, 1)
                dve.wait_ge(coef_step, done + 1)
                dve.tensor_tensor(cross[:], c, be, ALU.mult).then_inc(coef_step, 1)
                if n == 1:
                    dve.tensor_tensor(be, be, c, ALU.add).then_inc(coef_step, 1)
                    dve.wait_ge(coef_step, done + 2)
                    dve.tensor_scalar(al, cross[:], -1.0, 1.0, ALU.mult, ALU.add).then_inc(coef_step, 1)
                else:
                    dve.tensor_tensor(c, c, al, ALU.mult).then_inc(coef_step, 1)
                    dve.wait_ge(coef_step, done + 2)
                    dve.tensor_tensor(al, al, cross[:], ALU.subtract).then_inc(coef_step, 1)
                    dve.wait_ge(coef_step, done + 3)
                    dve.tensor_tensor(be, be, c, ALU.add).then_inc(coef_step, 1)

            def mix(b, n, j):
                k = ET * (((CYCLES - 1) * b + n - 1) * NJ + j)
                dve.wait_ge(coef_step, coef_steps(b, n - 1, j))

                def multiply(m):
                    if n == 1:
                        dve.tensor_tensor(u[j][:, m, :], Bt[j][:, m, :], beta[:, j, :], ALU.mult).then_inc(mul_ready, 1)
                    else:
                        dve.tensor_tensor(u[j][:, m, :], A[j][:, m, :], alpha[:, j, :], ALU.mult).then_inc(mul_ready, 1)

                def add(m):
                    dve.wait_ge(mul_ready, k + m + 1)
                    if n == 2:
                        dve.wait_ge(B_scaled, ET * (NJ * b + j) + m + 1)
                    other = A if n == 1 else Bt
                    dve.tensor_tensor(u[j][:, m, :], u[j][:, m, :], other[j][:, m, :], ALU.add).then_inc(u_ready, 1)

                multiply(0)
                for m in range(1, ET):
                    multiply(m)
                    add(m - 1)
                add(ET - 1)

            def gated_columns(b, j):
                k = NJ * b + j
                dve.wait_ge(cols_ps_ready, k + 1)
                dve.tensor_scalar(cols[:, j, :], tr[:, j, 0:2 * TT], gate_f[:], None, ALU.mult).then_inc(cols_ready, 1)
                dve.wait_ge(cols_ready, 2 * k + 1)
                dve.tensor_scalar(neg_cols[:, j, :], cols[:, j, TT:2 * TT], -1.0, None, ALU.mult).then_inc(cols_ready, 1)
                dve.wait_ge(cols_ready, 2 * k + 2)

            def finish(b, j, s):
                k = TT * (NJ * b + j) + s
                dve.scalar_tensor_tensor(u[j][:, s, :], xn[j][:, s, :], cols[:, j, s:s + 1], x1[j][:, s, :], ALU.mult, ALU.add).then_inc(y_base, 1)
                dve.wait_ge(y_base, k + 1)
                for t in range(ET):
                    source, sign = ((2, 1), (3, -1), (0, -1), (1, 1))[t]
                    beta_s = cols[:, j, TT + s:TT + s + 1] if sign > 0 else neg_cols[:, j, s:s + 1]
                    last = dve.scalar_tensor_tensor(u[j][:, s, t * P:(t + 1) * P], xn[j][:, s, source * P:(source + 1) * P], beta_s,
                                                    u[j][:, s, t * P:(t + 1) * P], ALU.mult, ALU.add)
                if s == TT - 1:
                    last.then_inc(y_ready, 1)

            def batch(b, first, more):
                def finish_before(s):
                    if not first:
                        finish(b - 1, 1, s)

                residual(b, 0, 0)
                residual(b, 0, 1)
                if not first:
                    gated_columns(b - 1, 1)
                finish_before(0)
                residual(b, 0, 2)
                finish_before(1)
                residual(b, 0, 3)
                mean_var(b, 0)
                finish_before(2)
                normalise(b, 0)
                if first:
                    prepare_weights()
                residual(b, 1, 0)
                residual(b, 1, 1)
                split_x(b, 0, (0, 1))
                finish_before(3)
                residual(b, 1, 2)
                split_x(b, 0, (2, 3))
                residual(b, 1, 3)
                mean_var(b, 1)
                normalise(b, 1)
                read_B(b, 0, 0)
                read_B(b, 0, 1)
                split_x(b, 1, (0, 1))
                read_B(b, 0, 2)
                split_x(b, 1, (2, 3))
                dve.wait_ge(xT_hi_ready, NJ * ET * (b + 1))
                dve.tensor_tensor(total[:], sums[:, 0, :], sums[:, 1, :], ALU.add).then_inc(total_ready, 1)
                read_B(b, 0, 3)
                read_B(b, 1, 0)
                read_B(b, 1, 1)
                if more:
                    split_attention(b + 1, 0, rinv)
                read_B(b, 1, 2)
                read_B(b, 1, 3)
                dve.wait_ge(g3_ready, b + 1)
                dve.tensor_scalar(base[:], g_tanh[:], range_7[:], BASE_COUPLING, ALU.mult, ALU.add).then_inc(base_ready, 1)
                for k in range(NJ * CYCLES):
                    n, j = k // NJ, k % NJ
                    coefficients(b, n, j)
                    if n < CYCLES - 1:
                        mix(b, n + 1, j)
                    elif j == 0:
                        gated_columns(b, 0)
                        for s in range(TT):
                            finish(b, 0, s)
                    if k == 0 and more:
                        split_attention(b + 1, 1, rinv)

            batches(dve, batch)
            gated_columns(B - 1, 1)
            for s in range(TT):
                finish(B - 1, 1, s)


INPUTS = ("x", "ctxT", "mask", "adj", "WqT", "bq", "WkT", "bk", "WvT", "g_xattn", "g_ffn", "bv", "WoT", "bo", "cn_w1", "cn_b1", "cn_w2",
          "cn_b2", "cn_w3", "cn_b3", "cn_w4", "cn_b4", "gc_w1", "gc_b1", "gc_w2", "gc_b2", "gc_w3", "gc_b3", "adaptive_range")


def gated_block(nc, x, ctxT, mask, adj, WqT, bq, WkT, bk, WvT, g_xattn, g_ffn, bv, WoT, bo, cn_w1, cn_b1, cn_w2, cn_b2, cn_w3, cn_b3,
                cn_w4, cn_b4, gc_w1, gc_b1, gc_w2, gc_b2, gc_w3, gc_b3, adaptive_range, out):
    def scratch(name, shape):
        return nc.dram_tensor(name, shape, F32, kind="Internal").ap()

    q_parts = scratch("q_parts", (2, E, TOK))
    k_parts = scratch("k_parts", (2, E, TOK))
    v_all = scratch("v_all", (TOK, E))
    o_all = scratch("o_all", (E, TOK))
    rinv_all = scratch("rinv_all", (B * H // HPG, HPG * S // P, P))
    with ExitStack() as ctx:
        am = ctx.enter_context(nc.sbuf_tensor("am", [P, S // P, S], F32))
        k_first = ctx.enter_context(nc.sbuf_tensor("k_first", [P, HPG, S], F32R))
        q_first = ctx.enter_context(nc.sbuf_tensor("q_first", [P, HPG, QB], F32R))
        v_first = ctx.enter_context(nc.sbuf_tensor("v_first", [P, S // P, P], F32))
        project_phase(nc, x, ctxT, WqT, bq, WkT, bk, WvT, adj, mask, q_parts, k_parts, v_all, am, k_first, q_first, v_first)
        attention_phase(nc, adj, mask, q_parts, k_parts, v_all, am, k_first, q_first, v_first, o_all, rinv_all)
    ffn_phase(nc, x, o_all, rinv_all, g_xattn, g_ffn, bv, WoT, bo, cn_w1, cn_b1, cn_w2, cn_b2, cn_w3, cn_b3, cn_w4, cn_b4,
              gc_w1, gc_b1, gc_w2, gc_b2, gc_w3, gc_b3, adaptive_range, out)


def kernel(x, ctx_1024, mask_Bx1xSxS2_ik1, g_xattn, g_ffn, L0_xattn_adj, L0_xattn_Wq, L0_xattn_bq, L0_xattn_Wk, L0_xattn_bk,
           L0_xattn_Wv, L0_xattn_bv, L0_xattn_Wo, L0_xattn_bo, L0_ffn_adaptive_range, **ffn):
    import concourse.bacc as bacc
    from concourse.bass_utils import run_bass_kernel_spmd

    arrays = dict(
        x=x.reshape(TOK, E), mask=mask_Bx1xSxS2_ik1.reshape(TOK, S), adj=L0_xattn_adj,
        ctxT=ctx_1024.reshape(NCH, CH, E).transpose(0, 2, 1),
        WqT=L0_xattn_Wq.T, WkT=L0_xattn_Wk.T, WvT=L0_xattn_Wv.T, WoT=L0_xattn_Wo.T,
        bq=L0_xattn_bq, bk=L0_xattn_bk, bv=L0_xattn_bv, bo=L0_xattn_bo, g_xattn=g_xattn, g_ffn=g_ffn,
        adaptive_range=L0_ffn_adaptive_range)
    arrays.update({name[len("L0_ffn_"):]: array for name, array in ffn.items()})
    arrays = {name: np.ascontiguousarray(arrays[name]) for name in INPUTS}

    nc = bacc.Bacc("TRN2", target_bir_lowering=False, num_devices=1)
    args = {name: nc.dram_tensor(name, a.shape, mybir.dt.from_np(a.dtype), kind="ExternalInput").ap() for name, a in arrays.items()}
    out = nc.dram_tensor("out", (TOK, E), F32, kind="ExternalOutput").ap()
    gated_block(nc, out=out, **args)
    result = run_bass_kernel_spmd(nc, [arrays], core_ids=[0])
    return result.results[0]["out"].reshape(B, S, E)
```
